# Optimizing a Trainium2 kernel written in Bass

```python
import numpy as np
import jax
import jax.numpy as jnp

def _softmax(x, axis=-1):
    return jax.nn.softmax(x, axis=axis)

def _gelu(x):
    return jax.nn.gelu(x, approximate=True)

def _silu(x):
    return jax.nn.silu(x)

def _sigmoid(x):
    return jax.nn.sigmoid(x)

def _layernorm(x, axis=-1, eps=1e-05):
    m = jnp.mean(x, axis=axis, keepdims=True)
    v = jnp.var(x, axis=axis, keepdims=True)
    return (x - m) / jnp.sqrt(v + eps)

def _scatter_add(tgt, idx, src, axis=0):
    return tgt.at[idx].add(src)

def _segment_sum(src, seg, n):
    return jax.ops.segment_sum(src, seg, n)
kernel_name = 'mk_xattn_seq_d1_seqx_r8_ee3dc8'

def setup_inputs(seed: int=0):
    np.random.seed(seed)
    _w = jnp.asarray

    def _rec_inputs():
        import jax
        import jax.numpy as jnp
        _rk = jax.random.key(seed)
        x = -0.0005207 + 1.001 * jax.random.normal(jax.random.fold_in(_rk, 1), (2, 256, 256), jnp.float32)
        _lenS = 256 - jax.random.randint(jax.random.fold_in(_rk, 7), (2,), 0, max(1, 256 // 4) + 1, jnp.int32)
        _lenS2 = 512 - jax.random.randint(jax.random.fold_in(_rk, 8), (2,), 0, max(1, 512 // 4) + 1, jnp.int32)
        _ctx_2048P = jax.random.normal(jax.random.fold_in(_rk, 11), (2, 16, 256), jnp.float32)
        _ctx_2048c = jax.random.dirichlet(jax.random.fold_in(_rk, 511), 0.3 * jnp.ones((16,), jnp.float32), (2, 512))
        _ctx_2048t = jnp.einsum('bsk,bkd->bsd', _ctx_2048c, _ctx_2048P)
        _ctx_2048t = _ctx_2048t * jax.lax.rsqrt(jnp.mean(jnp.square(_ctx_2048t)) + 1e-12) * 0.953939
        ctx_2048 = 2.81802e-05 + 1.00001 * (_ctx_2048t + 0.3 * jax.random.normal(jax.random.fold_in(_rk, 611), (2, 512, 256), jnp.float32))
        return (x, ctx_2048)
    x, ctx_2048 = _rec_inputs()

    def _L0_xattn_setup():
        import jax, jax.numpy as jnp
        import numpy as np
        B, Q, S1, S2 = (4, 32, 256, 256)
        D, H, K, F = (256, 16, 128, 1024)
        LN_EPS = 1e-05

        def _layer_norm(x, scale, offset):
            mu = jnp.mean(x, axis=-1, keepdims=True)
            var = jnp.var(x, axis=-1, keepdims=True)
            return (x - mu) * jax.lax.rsqrt(var + LN_EPS) * scale + offset

        def _cross_attention(q_in, kv_in, wq, bq, wk, bk, wv, bv, wo, bo, bias_k, bias_v):
            b, q_len, _ = q_in.shape
            t = kv_in.shape[1]
            qh = (q_in @ wq + bq).reshape(b, q_len, H, K)
            kh = (kv_in @ wk + bk).reshape(b, t, H, K)
            vh = (kv_in @ wv + bv).reshape(b, t, H, K)
            kh = jnp.concatenate([kh, jnp.broadcast_to(bias_k, (b, 1, H, K))], axis=1)
            vh = jnp.concatenate([vh, jnp.broadcast_to(bias_v, (b, 1, H, K))], axis=1)
            scale = jnp.sqrt(jnp.asarray(K, q_in.dtype))
            logits = jnp.einsum('bqhk,bthk->bhqt', qh, kh) / scale
            weights = jax.nn.softmax(logits, axis=-1)
            ctx = jnp.einsum('bhqt,bthk->bqhk', weights, vh).reshape(b, q_len, H * K)
            return ctx @ wo + bo

        def _forward(x, xf_1, xf_2, ln1_scale, ln1_offset, wq1, bq1, wk1, bk1, wv1, bv1, wo1, bo1, bias_k1, bias_v1, ln2_scale, ln2_offset, wq2, bq2, wk2, bk2, wv2, bv2, wo2, bo2, bias_k2, bias_v2, ln_mlp_scale, ln_mlp_offset, w_fc1, b_fc1, w_fc2, b_fc2):
            res = x
            h = _layer_norm(x, ln1_scale, ln1_offset)
            x = res + _cross_attention(h, xf_1, wq1, bq1, wk1, bk1, wv1, bv1, wo1, bo1, bias_k1, bias_v1)
            res = x
            h = _layer_norm(x, ln2_scale, ln2_offset)
            x = res + _cross_attention(h, xf_2, wq2, bq2, wk2, bk2, wv2, bv2, wo2, bo2, bias_k2, bias_v2)
            h = _layer_norm(x, ln_mlp_scale, ln_mlp_offset)
            h = jax.nn.gelu(h @ w_fc1 + b_fc1, approximate=False) @ w_fc2 + b_fc2
            return x + h
        key = jax.random.key(seed)
        ks = iter(jax.random.split(key, 64))

        def rn(shape, s=0.02):
            return jax.random.normal(next(ks), shape, jnp.float32) * s
        inp = {'x': rn((B, Q, D), 1.0), 'xf_1': rn((B, S1, D), 1.0), 'xf_2': rn((B, S2, D), 1.0)}
        for i in (1, 2):
            inp[f'ln{i}_scale'] = jnp.ones((D,), jnp.float32)
            inp[f'ln{i}_offset'] = jnp.zeros((D,), jnp.float32)
            inp[f'wq{i}'] = rn((D, H * K))
            inp[f'bq{i}'] = jnp.zeros((H * K,), jnp.float32)
            inp[f'wk{i}'] = rn((D, H * K))
            inp[f'bk{i}'] = jnp.zeros((H * K,), jnp.float32)
            inp[f'wv{i}'] = rn((D, H * K))
            inp[f'bv{i}'] = jnp.zeros((H * K,), jnp.float32)
            inp[f'wo{i}'] = rn((H * K, D))
            inp[f'bo{i}'] = jnp.zeros((D,), jnp.float32)
            inp[f'bias_k{i}'] = rn((1, 1, H, K))
            inp[f'bias_v{i}'] = rn((1, 1, H, K))
        inp['ln_mlp_scale'] = jnp.ones((D,), jnp.float32)
        inp['ln_mlp_offset'] = jnp.zeros((D,), jnp.float32)
        inp['w_fc1'] = rn((D, F))
        inp['b_fc1'] = jnp.zeros((F,), jnp.float32)
        inp['w_fc2'] = rn((F, D))
        inp['b_fc2'] = jnp.zeros((D,), jnp.float32)
        return inp
    _L0_xattn_all = _L0_xattn_setup()
    _L0_xattn_in = {k: v for k, v in _L0_xattn_all.items() if k in ('ln1_scale', 'ln1_offset', 'wq1', 'bq1', 'wk1', 'bk1', 'wv1', 'bv1', 'wo1', 'bo1', 'bias_k1', 'bias_v1', 'ln2_scale', 'ln2_offset', 'wq2', 'bq2', 'wk2', 'bk2', 'wv2', 'bv2', 'wo2', 'bo2', 'bias_k2', 'bias_v2', 'ln_mlp_scale', 'ln_mlp_offset', 'w_fc1', 'b_fc1', 'w_fc2', 'b_fc2')}
    del _L0_xattn_all
    return {'x': x, 'ctx_2048': ctx_2048, 'L0_xattn_ln1_scale': _L0_xattn_in['ln1_scale'], 'L0_xattn_ln1_offset': _L0_xattn_in['ln1_offset'], 'L0_xattn_wq1': _L0_xattn_in['wq1'], 'L0_xattn_bq1': _L0_xattn_in['bq1'], 'L0_xattn_wk1': _L0_xattn_in['wk1'], 'L0_xattn_bk1': _L0_xattn_in['bk1'], 'L0_xattn_wv1': _L0_xattn_in['wv1'], 'L0_xattn_bv1': _L0_xattn_in['bv1'], 'L0_xattn_wo1': _L0_xattn_in['wo1'], 'L0_xattn_bo1': _L0_xattn_in['bo1'], 'L0_xattn_bias_k1': _L0_xattn_in['bias_k1'], 'L0_xattn_bias_v1': _L0_xattn_in['bias_v1'], 'L0_xattn_ln2_scale': _L0_xattn_in['ln2_scale'], 'L0_xattn_ln2_offset': _L0_xattn_in['ln2_offset'], 'L0_xattn_wq2': _L0_xattn_in['wq2'], 'L0_xattn_bq2': _L0_xattn_in['bq2'], 'L0_xattn_wk2': _L0_xattn_in['wk2'], 'L0_xattn_bk2': _L0_xattn_in['bk2'], 'L0_xattn_wv2': _L0_xattn_in['wv2'], 'L0_xattn_bv2': _L0_xattn_in['bv2'], 'L0_xattn_wo2': _L0_xattn_in['wo2'], 'L0_xattn_bo2': _L0_xattn_in['bo2'], 'L0_xattn_bias_k2': _L0_xattn_in['bias_k2'], 'L0_xattn_bias_v2': _L0_xattn_in['bias_v2'], 'L0_xattn_ln_mlp_scale': _L0_xattn_in['ln_mlp_scale'], 'L0_xattn_ln_mlp_offset': _L0_xattn_in['ln_mlp_offset'], 'L0_xattn_w_fc1': _L0_xattn_in['w_fc1'], 'L0_xattn_b_fc1': _L0_xattn_in['b_fc1'], 'L0_xattn_w_fc2': _L0_xattn_in['w_fc2'], 'L0_xattn_b_fc2': _L0_xattn_in['b_fc2']}

def reference(x, ctx_2048, L0_xattn_ln1_scale, L0_xattn_ln1_offset, L0_xattn_wq1, L0_xattn_bq1, L0_xattn_wk1, L0_xattn_bk1, L0_xattn_wv1, L0_xattn_bv1, L0_xattn_wo1, L0_xattn_bo1, L0_xattn_bias_k1, L0_xattn_bias_v1, L0_xattn_ln2_scale, L0_xattn_ln2_offset, L0_xattn_wq2, L0_xattn_bq2, L0_xattn_wk2, L0_xattn_bk2, L0_xattn_wv2, L0_xattn_bv2, L0_xattn_wo2, L0_xattn_bo2, L0_xattn_bias_k2, L0_xattn_bias_v2, L0_xattn_ln_mlp_scale, L0_xattn_ln_mlp_offset, L0_xattn_w_fc1, L0_xattn_b_fc1, L0_xattn_w_fc2, L0_xattn_b_fc2):
    import jax
    import jax.numpy as jnp

    def _L0_xattn_ref(x, xf_1, xf_2, ln1_scale, ln1_offset, wq1, bq1, wk1, bk1, wv1, bv1, wo1, bo1, bias_k1, bias_v1, ln2_scale, ln2_offset, wq2, bq2, wk2, bk2, wv2, bv2, wo2, bo2, bias_k2, bias_v2, ln_mlp_scale, ln_mlp_offset, w_fc1, b_fc1, w_fc2, b_fc2):
        import jax, jax.numpy as jnp
        import numpy as np
        B, Q, S1, S2 = (4, 32, 256, 256)
        D, H, K, F = (256, 16, 128, 1024)
        LN_EPS = 1e-05

        def _layer_norm(x, scale, offset):
            mu = jnp.mean(x, axis=-1, keepdims=True)
            var = jnp.var(x, axis=-1, keepdims=True)
            return (x - mu) * jax.lax.rsqrt(var + LN_EPS) * scale + offset

        def _cross_attention(q_in, kv_in, wq, bq, wk, bk, wv, bv, wo, bo, bias_k, bias_v):
            b, q_len, _ = q_in.shape
            t = kv_in.shape[1]
            qh = (q_in @ wq + bq).reshape(b, q_len, H, K)
            kh = (kv_in @ wk + bk).reshape(b, t, H, K)
            vh = (kv_in @ wv + bv).reshape(b, t, H, K)
            kh = jnp.concatenate([kh, jnp.broadcast_to(bias_k, (b, 1, H, K))], axis=1)
            vh = jnp.concatenate([vh, jnp.broadcast_to(bias_v, (b, 1, H, K))], axis=1)
            scale = jnp.sqrt(jnp.asarray(K, q_in.dtype))
            logits = jnp.einsum('bqhk,bthk->bhqt', qh, kh) / scale
            weights = jax.nn.softmax(logits, axis=-1)
            ctx = jnp.einsum('bhqt,bthk->bqhk', weights, vh).reshape(b, q_len, H * K)
            return ctx @ wo + bo

        def _forward(x, xf_1, xf_2, ln1_scale, ln1_offset, wq1, bq1, wk1, bk1, wv1, bv1, wo1, bo1, bias_k1, bias_v1, ln2_scale, ln2_offset, wq2, bq2, wk2, bk2, wv2, bv2, wo2, bo2, bias_k2, bias_v2, ln_mlp_scale, ln_mlp_offset, w_fc1, b_fc1, w_fc2, b_fc2):
            res = x
            h = _layer_norm(x, ln1_scale, ln1_offset)
            x = res + _cross_attention(h, xf_1, wq1, bq1, wk1, bk1, wv1, bv1, wo1, bo1, bias_k1, bias_v1)
            res = x
            h = _layer_norm(x, ln2_scale, ln2_offset)
            x = res + _cross_attention(h, xf_2, wq2, bq2, wk2, bk2, wv2, bv2, wo2, bo2, bias_k2, bias_v2)
            h = _layer_norm(x, ln_mlp_scale, ln_mlp_offset)
            h = jax.nn.gelu(h @ w_fc1 + b_fc1, approximate=False) @ w_fc2 + b_fc2
            return x + h
        return _forward(x, xf_1, xf_2, ln1_scale, ln1_offset, wq1, bq1, wk1, bk1, wv1, bv1, wo1, bo1, bias_k1, bias_v1, ln2_scale, ln2_offset, wq2, bq2, wk2, bk2, wv2, bv2, wo2, bo2, bias_k2, bias_v2, ln_mlp_scale, ln_mlp_offset, w_fc1, b_fc1, w_fc2, b_fc2)
    x = _L0_xattn_ref(x, ctx_2048, ctx_2048, L0_xattn_ln1_scale, L0_xattn_ln1_offset, L0_xattn_wq1, L0_xattn_bq1, L0_xattn_wk1, L0_xattn_bk1, L0_xattn_wv1, L0_xattn_bv1, L0_xattn_wo1, L0_xattn_bo1, L0_xattn_bias_k1, L0_xattn_bias_v1, L0_xattn_ln2_scale, L0_xattn_ln2_offset, L0_xattn_wq2, L0_xattn_bq2, L0_xattn_wk2, L0_xattn_bk2, L0_xattn_wv2, L0_xattn_bv2, L0_xattn_wo2, L0_xattn_bo2, L0_xattn_bias_k2, L0_xattn_bias_v2, L0_xattn_ln_mlp_scale, L0_xattn_ln_mlp_offset, L0_xattn_w_fc1, L0_xattn_b_fc1, L0_xattn_w_fc2, L0_xattn_b_fc2)
    return x

_drawn_inputs = setup_inputs


def setup_inputs(seed=0):
    import zlib

    import numpy as np

    out = dict(_drawn_inputs(seed))
    spreads = {'L0_xattn_ln1_scale': (1.0, 0.6),
     'L0_xattn_ln1_offset': (0.0, 0.8),
     'L0_xattn_bq1': (0.0, 0.8),
     'L0_xattn_bk1': (0.0, 2.0),
     'L0_xattn_bv1': (0.0, 0.1),
     'L0_xattn_bo1': (0.0, 0.1),
     'L0_xattn_ln2_scale': (1.0, 0.6),
     'L0_xattn_ln2_offset': (0.0, 0.8),
     'L0_xattn_bq2': (0.0, 0.8),
     'L0_xattn_bk2': (0.0, 2.0),
     'L0_xattn_bv2': (0.0, 0.1),
     'L0_xattn_bo2': (0.0, 0.1),
     'L0_xattn_ln_mlp_scale': (1.0, 0.6),
     'L0_xattn_ln_mlp_offset': (0.0, 0.693),
     'L0_xattn_b_fc1': (0.0, 0.1),
     'L0_xattn_b_fc2': (0.0, 0.1)}
    factors = {'L0_xattn_wq1': 8.0,
     'L0_xattn_wk1': 8.0,
     'L0_xattn_bias_k1': 64.0,
     'L0_xattn_bias_v1': 64.0,
     'L0_xattn_wq2': 8.0,
     'L0_xattn_wk2': 8.0,
     'L0_xattn_bias_k2': 64.0,
     'L0_xattn_bias_v2': 64.0}
    for name, (base, spread) in spreads.items():
        noise = np.random.default_rng([zlib.crc32(name.encode()), seed]).standard_normal(out[name].shape)
        drawn = base * np.exp(spread * noise) if base else spread * noise
        out[name] = jnp.asarray(drawn.astype(out[name].dtype))
    for name, factor in factors.items():
        out[name] = (out[name] * factor).astype(out[name].dtype)
    return out
```

```python
from contextlib import ExitStack

import concourse.bass as bass
from concourse import mybir

F32 = mybir.dt.float32
F32R = mybir.dt.float32r
ALU = mybir.AluOpType
ACT = mybir.ActivationFunctionType
AX_X = mybir.AxisListType.X

P = 128
BATCH, QLEN, CLEN, D = 2, 256, 512, 256
HEADS, HD, F = 16, 128, 1024
LAYERS = 2
LN_EPS = 1e-5
SCALE = float(HD) ** -0.5

DC = D // P
TOK = BATCH * QLEN
QT = TOK // P
QTB = QLEN // P
CT = BATCH * CLEN // P
CTB = CLEN // P
PW = 2 * HD
PAIRS = HEADS // 2
ALL_PAIRS = LAYERS * PAIRS
FT = F // P
FB = F - PW
NORMS = LAYERS + 1
UNITS = [(0, 0), (0, 1), (1, 0), (1, 1)]
NU = len(UNITS)
NS = NU * QTB
NT = NU * 2
NK = 2 * BATCH
NQ = 2
NV = CT // 2
BQ, BK, BV, BIAS_K = 0, 1, 2, 3
CTX_BANK = 5
S_BANKS = [0, 1, 2, 3, 0, 1, 0, 1]
PT_BANKS = [3, 4, 3, 4, 2, 3, 0, 1]
K_BANKS = {"step": [4, 2, 0, 1], "prologue": [0, 1, 2, 3]}
Q_BANKS = {"step": [2, 4], "prologue": [4, 0]}
V_BANKS = {"step": [2, 3, 4, CTX_BANK], "prologue": [4, 0, 1, CTX_BANK]}
H_BANKS = {"prologue": [2, 3], "mlp": [0, 1]}
G_BANKS = [(f + 2) % 5 for f in range(FT)]
LOAD = 16


def build_program(nc, x_in, ctx_in, wq_in, wk_in, wv_in, wo_in, vrows_in, head_rows_in,
                  dim_rows_in, out_rows_in, wf1_in, wf2_in, out):
    with ExitStack() as stack:
        def sb(name, shape, dt=F32):
            return stack.enter_context(nc.sbuf_tensor(name, shape, dt))

        def sem(name):
            return stack.enter_context(nc.semaphore(name))

        ring = [stack.enter_context(nc.psum_tensor(f"ring{i}", [P, 512], F32)) for i in range(5)]
        ring.append(stack.enter_context(nc.psum_tensor("ps_ctx", [P, 512], F32)))
        ps_ctx = ring[CTX_BANK]
        acc = [stack.enter_context(nc.psum_tensor(f"acc{i}", [P, 512], F32)) for i in range(2)]

        ident = sb("ident", [P, P])
        zeros = sb("zeros", [P, 512], F32R)
        minus_half = sb("minus_half", [P, QT])
        head_rows = sb("head_rows", [P, P])
        dim_rows = sb("dim_rows", [20, P])
        head_cols = sb("head_cols", [P, 4, LAYERS * HEADS])
        step_cols = sb("step_cols", [P, ALL_PAIRS + 1, 3, 2])
        cols = sb("cols", [P, 3, 2])
        dim_cols = sb("dim_cols", [P, 20])
        out_rows = sb("out_rows", [P, NORMS, D])
        cT_hi = sb("cT_hi", [P, DC, CT * P], F32R)
        cT_lo = sb("cT_lo", [P, DC, CT * P], F32R)
        x_sb = sb("x_sb", [P, QT, D])
        x_res = sb("x_res", [P, QT, D])
        z_sb = sb("z_sb", [P, QT, D])
        h_full = sb("h_full", [P, DC, TOK])
        h_hi = sb("h_hi", [P, DC, TOK], F32R)
        h_lo = sb("h_lo", [P, DC, TOK], F32R)
        bn = sb("bn", [P, QT, 6])
        mean_var = sb("mean_var", [P, QT, 2])
        var_eps = sb("var_eps", [P, QT])
        rstd = sb("rstd", [P, QT])
        wq_raw = sb("wq_raw", [P, DC, PW])
        wk_raw = sb("wk_raw", [P, DC, PW])
        wv_raw = sb("wv_raw", [P, DC, PW])
        wo_raw = sb("wo_raw", [P, 2, D])
        wq_hi, wq_lo = sb("wq_hi", [P, DC, PW], F32R), sb("wq_lo", [P, DC, PW], F32R)
        wk_hi, wk_lo = sb("wk_hi", [P, DC, PW], F32R), sb("wk_lo", [P, DC, PW], F32R)
        wv_hi, wv_lo = sb("wv_hi", [P, DC, PW], F32R), sb("wv_lo", [P, DC, PW], F32R)
        wo_hi, wo_lo = sb("wo_hi", [P, 2, D], F32R), sb("wo_lo", [P, 2, D], F32R)
        vrows = sb("vrows", [P, 2, PW])
        vbias = sb("vbias", [P, PW])
        q_hi, q_lo = sb("q_hi", [P, 2, TOK], F32R), sb("q_lo", [P, 2, TOK], F32R)
        k_hi, k_lo = sb("k_hi", [P, 2, CT * P], F32R), sb("k_lo", [P, 2, CT * P], F32R)
        v_sum = sb("v_sum", [P, 2, 2 * PW])
        v_hi, v_lo = sb("v_hi", [P, CT, PW], F32R), sb("v_lo", [P, CT, PW], F32R)
        probs = sb("probs", [P, NU, QTB, CLEN])
        row_max = sb("row_max", [P, NU, QTB])
        shift = sb("shift", [P, NU, QTB])
        p_learned = sb("p_learned", [P, NU, QTB])
        row_sum = sb("row_sum", [P, NU, QTB])
        total = sb("total", [P, NU, QTB])
        inv = sb("inv", [P, NU, QTB])
        pT_hi, pT_lo = sb("pT_hi", [P, CTB, QLEN], F32R), sb("pT_lo", [P, CTB, QLEN], F32R)
        o_hi, o_lo = sb("o_hi", [P, 2, TOK], F32R), sb("o_lo", [P, 2, TOK], F32R)
        wf_raw = sb("wf_raw", [P, 2, 512])
        wf1_hi, wf1_lo = sb("wf1_hi", [P, DC, FB], F32R), sb("wf1_lo", [P, DC, FB], F32R)
        wf2_hi, wf2_lo = sb("wf2_hi", [P, FT, D], F32R), sb("wf2_lo", [P, FT, D], F32R)

        g_full = v_sum
        c_raw = probs[:].rearrange("p u q t -> p (u q t)")[:, 0:CT * D].rearrange("p (t d) -> p t d", d=D)

        def hidden(part_k, part_v, f):
            if f < FT // 2:
                return part_k[:].rearrange("p h t -> p (h t)")[:, f * 512:(f + 1) * 512]
            return part_v[:].rearrange("p t c -> p (t c)")[:, (f - FT // 2) * 512:(f - FT // 2 + 1) * 512]

        c_loaded = [sem(f"c_loaded{b}") for b in range(BATCH)]
        x_loaded, rows_loaded, out_rows_loaded = sem("x_loaded"), sem("rows_loaded"), sem("out_rows_loaded")
        wq_loaded, wk_loaded, wv_loaded, wo_loaded = (sem(f"w{n}_loaded") for n in "qkvo")
        wq_split, wk_split, wv_split, wo_split = (sem(f"w{n}_split") for n in "qkvo")
        wq_rounded, wk_rounded, wv_rounded, wo_rounded = (sem(f"w{n}_rounded") for n in "qkvo")
        wf_loaded = [sem(f"wf_loaded{i}") for i in range(2)]
        wf_rounded, wf_split = sem("wf_rounded"), sem("wf_split")
        ident_ready, zeros_ready = sem("ident_ready"), sem("zeros_ready")
        cT_filled, cT_rounded, cT_split = sem("cT_filled"), sem("cT_rounded"), sem("cT_split")
        cols_filled, cols_copied, cols_ready = sem("cols_filled"), sem("cols_copied"), sem("cols_ready")
        x_ready, bn_done, stats_ready = sem("x_ready"), sem("bn_done"), sem("stats_ready")
        eps_added, rstd_ready, z_ready = sem("eps_added"), sem("rstd_ready"), sem("z_ready")
        h_filled, h_drained, h_rounded, h_split = (sem(f"h_{n}") for n in ("filled", "drained", "rounded", "split"))
        res_ready = sem("res_ready")
        k_filled, k_rounded, k_split = sem("k_filled"), sem("k_rounded"), sem("k_split")
        q_filled, q_rounded, q_split = sem("q_filled"), sem("q_rounded"), sem("q_split")
        v_filled, v_summed, v_rounded, v_split = (sem(f"v_{n}") for n in ("filled", "summed", "rounded", "split"))
        s_filled, max_done, shift_ready = sem("s_filled"), sem("max_done"), sem("shift_ready")
        exp_done, total_done, inv_ready, p_ready = sem("exp_done"), sem("total_done"), sem("inv_ready"), sem("p_ready")
        pT_filled, pT_rounded, pT_split = sem("pT_filled"), sem("pT_rounded"), sem("pT_split")
        o_filled, o_rounded, o_split = sem("o_filled"), sem("o_rounded"), sem("o_split")
        acc_filled = sem("acc_filled")
        g_filled, gelu_done, g_rounded, g_split = (sem(f"g_{n}") for n in ("filled", "gelu", "rounded", "split"))
        passed, stored = sem("passed"), sem("stored")

        block = stack.enter_context(nc.Block())

        @block.sync
        def _(sp):
            def load_wk(n):
                sp.dma_start(wk_raw[:], wk_in[:, bass.ds(n * PW, PW)].rearrange("(c p) n -> p c n", p=P)).then_inc(wk_loaded, LOAD)

            def load_wq(n):
                sp.dma_start(wq_raw[:], wq_in[:, bass.ds(n * PW, PW)].rearrange("(c p) n -> p c n", p=P)).then_inc(wq_loaded, LOAD)

            def load_wv(n):
                sp.dma_start(wv_raw[:], wv_in[:, bass.ds(n * PW, PW)].rearrange("(c p) n -> p c n", p=P)).then_inc(wv_loaded, LOAD)
                sp.dma_start(vrows[:], vrows_in[:, bass.ds(n * PW, PW)].rearrange("(o r) n -> o r n", o=1).to_broadcast([P, 2, PW])).then_inc(wv_loaded, LOAD)

            def load_wo(n):
                sp.dma_start(wo_raw[:], wo_in[bass.ds(n * PW, PW), :].rearrange("(h p) n -> p h n", p=P)).then_inc(wo_loaded, LOAD)

            c_view = ctx_in.rearrange("b (t p) d -> p (b t) d", p=P)
            for b in range(BATCH):
                tiles = slice(CTB * b, CTB * (b + 1))
                sp.dma_start(c_raw[:, tiles, :], c_view[:, tiles, :]).then_inc(c_loaded[b], LOAD)
                if b == 0:
                    load_wk(0)
            sp.dma_start(head_rows[:], head_rows_in).then_inc(rows_loaded, LOAD)
            sp.dma_start(dim_rows[:], dim_rows_in).then_inc(rows_loaded, LOAD)
            sp.dma_start(x_sb[:], x_in.rearrange("b (t p) d -> p (b t) d", p=P)).then_inc(x_loaded, LOAD)
            load_wv(0)
            load_wq(0)
            load_wo(0)
            sp.dma_start(out_rows[:], out_rows_in.rearrange("(o r) n -> o r n", o=1).to_broadcast([P, NORMS, D])).then_inc(out_rows_loaded, LOAD)
            sp.wait_ge(wk_split, 1)
            load_wk(1)
            sp.wait_ge(wv_split, 1)
            load_wv(1)
            sp.wait_ge(wq_split, 1)
            load_wq(1)
            sp.wait_ge(wk_split, 2)
            load_wk(2)

            def refill(pair, wq=True, wk=True):
                if wq:
                    sp.wait_ge(wq_split, pair + 2)
                    load_wq(pair + 2)
                    sp.wait_ge(wv_split, pair + 2)
                    load_wv(pair + 2)
                sp.wait_ge(wo_split, pair + 1)
                load_wo(pair + 1)
                if wk:
                    sp.wait_ge(wk_split, pair + 3)
                    load_wk(pair + 3)

            def load_mlp(part):
                if part < 3:
                    src = wf1_in[:, PW * part:PW * (part + 1)].rearrange("(c p) n -> p c n", p=P)
                    dst = wf_raw[:, part % 2, :].rearrange("p (c n) -> p c n", c=DC)
                else:
                    src = wf2_in[PW * (part - 3):PW * (part - 2), :].rearrange("(f p) n -> p f n", p=P)
                    dst = wf_raw[:, part % 2, :].rearrange("p (f n) -> p f n", n=D)
                if part >= 2:
                    sp.wait_ge(wf_split, part - 1)
                sp.dma_start(dst, src).then_inc(wf_loaded[part % 2], LOAD)

            load_mlp(0)
            load_mlp(1)
            with sp.Fori(0, PAIRS - 1) as pair:
                refill(pair)
            for part in range(2, 7):
                load_mlp(part)
            with sp.Fori(PAIRS - 1, ALL_PAIRS - 2) as pair:
                refill(pair)
            refill(ALL_PAIRS - 2, wq=False, wk=False)

            for t in range(QT):
                if t % 2 == 0:
                    sp.wait_ge(x_ready, 2 * LAYERS + 1 + t // 2)
                sp.dma_start(out.rearrange("b (t p) d -> p (b t) d", p=P)[:, t, :], x_sb[:, t, :]).then_inc(stored, LOAD)
            sp.wait_ge(stored, QT * LOAD)

        @block.gpsimd
        def _(pool):
            def hold(semaphore, value):
                pool.wait_ge(semaphore, value)
                pool.sem_inc(passed, 1)

            def split_tile(raw, hi, lo, rounded, n, done):
                pool.tensor_scalar(hi, raw, 1.0, 0.0, ALU.mult, ALU.add).then_inc(rounded, 1)
                pool.wait_ge(rounded, n)
                pool.tensor_tensor(lo, raw, hi.bitcast(F32), ALU.subtract).then_inc(done, 1)

            def split_wk(n):
                hold(wk_loaded, (n + 1) * LOAD)
                split_tile(wk_raw[:], wk_hi[:], wk_lo[:], wk_rounded, n + 1, wk_split)

            def split_wq(n):
                hold(wq_loaded, (n + 1) * LOAD)
                split_tile(wq_raw[:], wq_hi[:], wq_lo[:], wq_rounded, n + 1, wq_split)

            def split_wv(n):
                pool.wait_ge(wv_loaded, (2 * n + 2) * LOAD)
                pool.tensor_tensor(vbias[:], vrows[:, 0, :], vrows[:, 1, :], ALU.subtract)
                split_tile(wv_raw[:], wv_hi[:], wv_lo[:], wv_rounded, n + 1, wv_split)

            def split_wo(n):
                hold(wo_loaded, (n + 1) * LOAD)
                split_tile(wo_raw[:], wo_hi[:], wo_lo[:], wo_rounded, n + 1, wo_split)

            def split_mlp(part):
                pool.wait_ge(wf_loaded[part % 2], (part // 2 + 1) * LOAD)
                if part < 3:
                    hi = wf1_hi[:, :, PW * part:PW * (part + 1)]
                    lo = wf1_lo[:, :, PW * part:PW * (part + 1)]
                    raw = wf_raw[:, part % 2, :].rearrange("p (c n) -> p c n", c=DC)
                else:
                    f = 2 * (part - 3)
                    hi, lo = wf2_hi[:, f:f + 2, :], wf2_lo[:, f:f + 2, :]
                    raw = wf_raw[:, part % 2, :].rearrange("p (f n) -> p f n", n=D)
                split_tile(raw, hi, lo, wf_rounded, part + 1, wf_split)

            def inverse_deviation(norm):
                pool.wait_ge(stats_ready, norm + 1)
                pool.tensor_scalar(var_eps[:], mean_var[:, :, 1], 1.0, LN_EPS, ALU.mult, ALU.add).then_inc(eps_added, 1)
                pool.wait_ge(eps_added, norm + 1)
                pool.tensor_tensor(rstd[:], var_eps[:], minus_half[:], ALU.pow).then_inc(rstd_ready, 1)

            def residual(norm):
                rows = out_rows[:, norm:norm + 1, :].to_broadcast([P, QT, D])
                pool.tensor_tensor(x_res[:], x_sb[:], rows, ALU.add).then_inc(res_ready, 1)

            def value_rest(pair, m):
                pool.wait_ge(v_rounded, NV * pair + m + 1)
                pool.tensor_tensor(v_lo[:, 2 * m:2 * m + 2, :], v_sum[:, m % 2, :].rearrange("p (t c) -> p t c", c=PW),
                                   v_hi[:, 2 * m:2 * m + 2, :].bitcast(F32), ALU.subtract).then_inc(v_split, 1)

            def normalise(pair, u):
                hold(inv_ready, NU * pair + u + 1)
                for q in range(QTB):
                    pool.tensor_scalar(probs[:, u, q, :], probs[:, u, q, :], inv[:, u, q:q + 1], 0.0, ALU.mult, ALU.add).then_inc(p_ready, 1)

            pool.memset(ident[:], 0.0).then_inc(ident_ready, 1)
            pool.memset(minus_half[:], -0.5)
            pool.wait_ge(ident_ready, 1)
            pool.affine_select(out=ident[:], in_=ident[:], compare_op=ALU.not_equal, fill=1.0, base=0,
                               pattern=[[-1, P]], channel_multiplier=1).then_inc(ident_ready, 1)
            pool.memset(zeros[:].bitcast(F32), 0.0).then_inc(zeros_ready, 1)
            split_wk(0)
            pool.wait_ge(cols_copied, 2)
            by_pair = head_cols[:].rearrange("p g (n h) -> p g n h", h=2)
            pool.memset(step_cols[:, 0, BV, :], 0.0)
            pool.memset(step_cols[:, ALL_PAIRS, 0:2, :], 0.0)
            pool.tensor_tensor(step_cols[:, 0:ALL_PAIRS, BK, :], by_pair[:, BK], by_pair[:, BIAS_K], ALU.subtract)
            pool.tensor_copy(step_cols[:, 0:ALL_PAIRS, BQ, :], by_pair[:, BQ])
            pool.tensor_copy(step_cols[:, 1:ALL_PAIRS + 1, BV, :], by_pair[:, BV]).then_inc(cols_ready, 1)

            def prologue(layer):
                first = PAIRS * layer
                if layer == 0:
                    split_wv(0)
                    inverse_deviation(layer)
                    split_wq(0)
                else:
                    inverse_deviation(layer)
                pool.wait_ge(k_filled, NK * (first + 1))
                split_wk(first + 1)
                for m in range(NV):
                    value_rest(first, m)
                if layer == 0:
                    pool.wait_ge(out_rows_loaded, LOAD)
                residual(layer)

            def step(pair, last=False, final=False):
                if not final:
                    pool.wait_ge(q_filled, NQ * (pair + 1))
                    split_wq(pair + 1)
                normalise(pair, 0)
                normalise(pair, 1)
                if not final:
                    pool.wait_ge(v_summed, NV * (pair + 1))
                    split_wv(pair + 1)
                normalise(pair, 2)
                pool.wait_ge(s_filled, NS * pair + 1)
                split_wo(pair)
                normalise(pair, 3)
                if not last:
                    pool.wait_ge(k_filled, NK * (pair + 2))
                    split_wk(pair + 2)
                    for m in range(NV):
                        value_rest(pair + 1, m)

            prologue(0)
            with pool.Fori(0, PAIRS - 1) as pair:
                step(pair)
            for part in range(3):
                split_mlp(part)
            step(PAIRS - 1, last=True)
            prologue(1)
            for part in range(3, 7):
                split_mlp(part)
            with pool.Fori(PAIRS, ALL_PAIRS - 1) as pair:
                step(pair)
            step(ALL_PAIRS - 1, last=True, final=True)
            inverse_deviation(LAYERS)
            residual(LAYERS)


        @block.scalar
        def _(act):
            def column(group, pair, h, where):
                return cols[:, group, h:h + 1] if where == "step" else step_cols[:, pair, group, h:h + 1]

            def round_k(pair, j, where):
                h, b = divmod(j, BATCH)
                act.wait_ge(k_filled, NK * pair + j + 1)
                act.activation(k_hi[:, h, b * CLEN:(b + 1) * CLEN], ring[K_BANKS[where][j]][:], ACT.Identity,
                               bias=column(BK, pair, h, where)).then_inc(k_rounded, 1)

            def round_q(pair, h, where):
                act.wait_ge(q_filled, NQ * pair + h + 1)
                act.activation(q_hi[:, h, :], ring[Q_BANKS[where][h]][:], ACT.Identity,
                               bias=column(BQ, pair, h, where)).then_inc(q_rounded, 1)

            def round_v(pair, m):
                act.wait_ge(v_summed, NV * pair + m + 1)
                act.activation(v_hi[:, 2 * m:2 * m + 2, :], v_sum[:, m % 2, :].rearrange("p (t c) -> p t c", c=PW),
                               ACT.Copy).then_inc(v_rounded, 1)

            def round_pT(pair, j):
                half = j % 2
                act.wait_ge(pT_filled, NT * pair + j + 1)
                act.activation(pT_hi[:, 2 * half:2 * half + 2, :], ring[PT_BANKS[j]][:].rearrange("p (t q) -> p t q", q=QLEN),
                               ACT.Copy).then_inc(pT_rounded, 1)

            def round_o(pair, u):
                h, b = UNITS[u]
                act.wait_ge(o_filled, NU * pair + u + 1)
                act.activation(o_hi[:, h, b * QLEN:(b + 1) * QLEN], ps_ctx[:, 0:QLEN], ACT.Identity,
                               bias=cols[:, BV, h:h + 1]).then_inc(o_rounded, 1)

            def exponentials(pair, u):
                act.wait_ge(shift_ready, NU * pair + u + 1)
                act.activation(p_learned[:, u, :], shift[:, u, :], ACT.Exp)
                for q in range(QTB):
                    act.activation(probs[:, u, q, :], ring[S_BANKS[QTB * u + q]][:], ACT.Exp, bias=shift[:, u, q:q + 1],
                                   scale=SCALE, accum_out=row_sum[:, u, q:q + 1]).then_inc(exp_done, 1)

            def round_h(norm):
                for c in range(DC):
                    act.wait_ge(h_drained, DC * norm + c + 1)
                    act.activation(h_hi[:, c, :], h_full[:, c, :], ACT.Copy).then_inc(h_rounded, 1)

            def prologue(layer):
                first = PAIRS * layer
                for j in range(NK):
                    round_k(first, j, "prologue")
                for m in range(NV):
                    round_v(first, m)
                round_h(layer)
                for h in range(NQ):
                    round_q(first, h, "prologue")

            def step(pair, last=False):
                exponentials(pair, 0)
                exponentials(pair, 1)
                if not last:
                    round_k(pair + 1, 0, "step")
                exponentials(pair, 2)
                if not last:
                    round_k(pair + 1, 1, "step")
                round_pT(pair, 0)
                round_pT(pair, 1)
                exponentials(pair, 3)
                if not last:
                    round_q(pair + 1, 0, "step")
                round_o(pair, 0)
                round_pT(pair, 2)
                round_pT(pair, 3)
                if not last:
                    round_k(pair + 1, 2, "step")
                    round_k(pair + 1, 3, "step")
                round_o(pair, 1)
                round_pT(pair, 4)
                round_pT(pair, 5)
                if not last:
                    round_q(pair + 1, 1, "step")
                round_o(pair, 2)
                round_pT(pair, 6)
                round_pT(pair, 7)
                if not last:
                    round_v(pair + 1, 0)
                    round_v(pair + 1, 1)
                round_o(pair, 3)
                if not last:
                    round_v(pair + 1, 2)
                    round_v(pair + 1, 3)

            for j in range(DC * BATCH):
                b, c = divmod(j, DC)
                act.wait_ge(cT_filled, j + 1)
                act.activation(cT_hi[:, c, b * CLEN:(b + 1) * CLEN], ring[j][:], ACT.Copy).then_inc(cT_rounded, 1)
            act.wait_ge(cols_ready, 1)
            for layer in range(LAYERS):
                prologue(layer)
                with act.Fori(PAIRS * layer, PAIRS * (layer + 1) - 1) as pair:
                    step(pair)
                step(PAIRS * (layer + 1) - 1, last=True)
            round_h(LAYERS)
            for f in range(FT):
                act.wait_ge(g_filled, f + 1)
                if f >= 2:
                    act.wait_ge(g_split, f - 1)
                act.activation(g_full[:, f % 2, :], ring[G_BANKS[f]][:], ACT.Gelu,
                               bias=dim_cols[:, 4 * NORMS + f:4 * NORMS + f + 1]).then_inc(gelu_done, 1)

        @block.vector
        def _(dve):
            def column(group, pair, h, where):
                return cols[:, group, h:h + 1] if where == "step" else step_cols[:, pair, group, h:h + 1]

            def split_k(pair, j, where):
                h, b = divmod(j, BATCH)
                part = slice(b * CLEN, (b + 1) * CLEN)
                dve.wait_ge(k_rounded, NK * pair + j + 1)
                dve.scalar_tensor_tensor(out=k_lo[:, h, part], in0=ring[K_BANKS[where][j]][:],
                                         scalar=column(BK, pair, h, where),
                                         in1=k_hi[:, h, part].bitcast(F32), op0=ALU.add, op1=ALU.subtract).then_inc(k_split, 1)

            def split_q(pair, h, where):
                dve.wait_ge(q_rounded, NQ * pair + h + 1)
                dve.scalar_tensor_tensor(out=q_lo[:, h, :], in0=ring[Q_BANKS[where][h]][:],
                                         scalar=column(BQ, pair, h, where),
                                         in1=q_hi[:, h, :].bitcast(F32), op0=ALU.add, op1=ALU.subtract).then_inc(q_split, 1)

            def sum_v(pair, m, where):
                dve.wait_ge(v_filled, NV * pair + m + 1)
                if not isinstance(pair, int) or NV * pair + m >= 2:
                    dve.wait_ge(v_split, NV * pair + m - 1)
                dve.tensor_tensor(v_sum[:, m % 2, :].rearrange("p (t c) -> p t c", c=PW),
                                  ring[V_BANKS[where][m]][:].rearrange("p (t c) -> p t c", c=PW),
                                  vbias[:].rearrange("p (o c) -> p o c", o=1).to_broadcast([P, 2, PW]), ALU.add).then_inc(v_summed, 1)

            def split_pT(pair, j):
                half = j % 2
                dve.wait_ge(pT_rounded, NT * pair + j + 1)
                dve.tensor_tensor(pT_lo[:, 2 * half:2 * half + 2, :], ring[PT_BANKS[j]][:].rearrange("p (t q) -> p t q", q=QLEN),
                                  pT_hi[:, 2 * half:2 * half + 2, :].bitcast(F32), ALU.subtract).then_inc(pT_split, 1)

            def split_o(pair, u):
                h, b = UNITS[u]
                part = slice(b * QLEN, (b + 1) * QLEN)
                dve.wait_ge(o_rounded, NU * pair + u + 1)
                dve.scalar_tensor_tensor(out=o_lo[:, h, part], in0=ps_ctx[:, 0:QLEN],
                                         scalar=cols[:, BV, h:h + 1],
                                         in1=o_hi[:, h, part].bitcast(F32), op0=ALU.add, op1=ALU.subtract).then_inc(o_split, 1)

            def maxima(pair, u):
                for q in range(QTB):
                    dve.wait_ge(s_filled, NS * pair + QTB * u + q + 1)
                    dve.reduce_max(row_max[:, u, q:q + 1], ring[S_BANKS[QTB * u + q]][:], AX_X).then_inc(max_done, 1)
                dve.wait_ge(max_done, NS * pair + QTB * (u + 1))
                dve.tensor_scalar(shift[:, u, :], row_max[:, u, :], -SCALE, 0.0, ALU.mult, ALU.min).then_inc(shift_ready, 1)

            def inverse_sums(pair, u):
                dve.wait_ge(exp_done, NS * pair + QTB * (u + 1))
                dve.tensor_tensor(total[:, u, :], row_sum[:, u, :], p_learned[:, u, :], ALU.add).then_inc(total_done, 1)
                dve.wait_ge(total_done, NU * pair + u + 1)
                dve.reciprocal(inv[:, u, :], total[:, u, :]).then_inc(inv_ready, 1)

            def new_x(n):
                dve.wait_ge(acc_filled, n + 1)
                dve.wait_ge(res_ready, n + 1)
                for a in range(2):
                    dve.tensor_tensor(x_sb[:, 2 * a:2 * a + 2, :], acc[a][:].rearrange("p (t d) -> p t d", d=D),
                                      x_res[:, 2 * a:2 * a + 2, :], ALU.add).then_inc(x_ready, 1)
                dve.wait_ge(x_ready, 2 * (n + 1))

            def stats(norm):
                for t in range(QT):
                    dve.bn_stats(bn[:, t, :], x_sb[:, t, :]).then_inc(bn_done, 1)
                dve.wait_ge(bn_done, QT * (norm + 1))
                for t in range(QT):
                    agg = dve.bn_aggr(mean_var[:, t, :], bn[:, t, :])
                agg.then_inc(stats_ready, 1)

            def standardise(norm):
                dve.wait_ge(stats_ready, norm + 1)
                dve.wait_ge(rstd_ready, norm + 1)
                for t in range(QT):
                    dve.tensor_scalar(z_sb[:, t, :], x_sb[:, t, :], mean_var[:, t, 0:1], rstd[:, t:t + 1],
                                      ALU.subtract, ALU.mult).then_inc(z_ready, 1)

            def scale_h(norm, where):
                for c in range(DC):
                    dve.wait_ge(h_filled, DC * norm + c + 1)
                    dve.tensor_scalar(h_full[:, c, :], ring[H_BANKS[where][c]][:], dim_cols[:, 4 * norm + c:4 * norm + c + 1],
                                      dim_cols[:, 4 * norm + DC + c:4 * norm + DC + c + 1], ALU.mult, ALU.add).then_inc(h_drained, 1)
                for c in range(DC):
                    dve.wait_ge(h_rounded, DC * norm + c + 1)
                    dve.tensor_tensor(h_lo[:, c, :], h_full[:, c, :], h_hi[:, c, :].bitcast(F32), ALU.subtract).then_inc(h_split, 1)

            def prologue(layer):
                first = PAIRS * layer
                if layer == 0:
                    dve.wait_ge(x_loaded, LOAD)
                else:
                    new_x(layer - 1)
                stats(layer)
                split_k(first, 0, "prologue")
                split_k(first, 1, "prologue")
                standardise(layer)
                split_k(first, 2, "prologue")
                split_k(first, 3, "prologue")
                dve.wait_ge(wv_split, first + 1)
                for m in range(NV):
                    sum_v(first, m, "prologue")
                scale_h(layer, "prologue")
                for h in range(NQ):
                    split_q(first, h, "prologue")

            def step(pair, last=False):
                dve.tensor_copy(cols[:].rearrange("p g h -> p (g h)"),
                                step_cols[:, bass.ds(pair + 1, 1), :, :].rearrange("p n g h -> p (n g h)"))
                maxima(pair, 0)
                maxima(pair, 1)
                inverse_sums(pair, 0)
                maxima(pair, 2)
                if not last:
                    split_k(pair + 1, 0, "step")
                inverse_sums(pair, 1)
                inverse_sums(pair, 2)
                if not last:
                    split_k(pair + 1, 1, "step")
                split_pT(pair, 0)
                split_pT(pair, 1)
                maxima(pair, 3)
                if not last:
                    split_q(pair + 1, 0, "step")
                inverse_sums(pair, 3)
                split_o(pair, 0)
                split_pT(pair, 2)
                split_pT(pair, 3)
                if not last:
                    split_k(pair + 1, 2, "step")
                    split_k(pair + 1, 3, "step")
                split_o(pair, 1)
                split_pT(pair, 4)
                split_pT(pair, 5)
                if not last:
                    split_q(pair + 1, 1, "step")
                split_o(pair, 2)
                split_pT(pair, 6)
                split_pT(pair, 7)
                if not last:
                    dve.wait_ge(wv_split, pair + 2)
                    sum_v(pair + 1, 0, "step")
                    sum_v(pair + 1, 1, "step")
                split_o(pair, 3)
                if not last:
                    sum_v(pair + 1, 2, "step")
                    sum_v(pair + 1, 3, "step")

            for j in range(DC * BATCH):
                b, c = divmod(j, DC)
                part = slice(b * CLEN, (b + 1) * CLEN)
                dve.wait_ge(cT_rounded, j + 1)
                dve.tensor_tensor(cT_lo[:, c, part], ring[j][:], cT_hi[:, c, part].bitcast(F32), ALU.subtract).then_inc(cT_split, 1)
            dve.wait_ge(cols_filled, 1)
            dve.tensor_copy(head_cols[:].rearrange("p g c -> p (g c)"), ring[4][:, 0:P]).then_inc(cols_copied, 1)
            dve.tensor_copy(dim_cols[:], ring[4][:, P:P + 20]).then_inc(cols_copied, 1)
            dve.wait_ge(cols_ready, 1)
            for layer in range(LAYERS):
                prologue(layer)
                with dve.Fori(PAIRS * layer, PAIRS * (layer + 1) - 1) as pair:
                    step(pair)
                step(PAIRS * (layer + 1) - 1, last=True)
            new_x(LAYERS - 1)
            stats(LAYERS)
            standardise(LAYERS)
            scale_h(LAYERS, "mlp")
            for f in range(FT):
                dve.wait_ge(gelu_done, f + 1)
                dve.tensor_copy(hidden(k_hi, v_hi, f), g_full[:, f % 2, :]).then_inc(g_rounded, 1)
                dve.wait_ge(g_rounded, f + 1)
                dve.tensor_tensor(hidden(k_lo, v_lo, f), g_full[:, f % 2, :], hidden(k_hi, v_hi, f).bitcast(F32),
                                  ALU.subtract).then_inc(g_split, 1)
            new_x(LAYERS)

        @block.tensor
        def _(pe):
            def product(out_ap, terms, start=True, stop=True):
                passes = [(a, b) for lhs_hi, lhs_lo, rhs_hi, rhs_lo in terms
                          for a, b in ((lhs_hi, rhs_lo), (lhs_lo, rhs_hi), (lhs_hi, rhs_hi))]
                for i, (a, b) in enumerate(passes):
                    ins = pe.matmul(out_ap, a, b, start=start and i == 0, stop=stop and i == len(passes) - 1)
                return ins

            def project_k(j, where):
                h, b = divmod(j, BATCH)
                cols, part = slice(h * HD, (h + 1) * HD), slice(b * CLEN, (b + 1) * CLEN)
                product(ring[K_BANKS[where][j]][:], [(wk_hi[:, c, cols], wk_lo[:, c, cols], cT_hi[:, c, part], cT_lo[:, c, part])
                                                     for c in range(DC)]).then_inc(k_filled, 1)

            def project_q(h, where):
                cols = slice(h * HD, (h + 1) * HD)
                product(ring[Q_BANKS[where][h]][:], [(wq_hi[:, c, cols], wq_lo[:, c, cols], h_hi[:, c, :], h_lo[:, c, :])
                                                     for c in range(DC)]).then_inc(q_filled, 1)

            def project_v(m, where):
                for i in range(2):
                    toks = slice((2 * m + i) * P, (2 * m + i + 1) * P)
                    last = product(ring[V_BANKS[where][m]][:, i * PW:(i + 1) * PW],
                                   [(cT_hi[:, c, toks], cT_lo[:, c, toks], wv_hi[:, c, :], wv_lo[:, c, :]) for c in range(DC)])
                last.then_inc(v_filled, 1)

            def scores(u, q):
                h, b = UNITS[u]
                toks, part = slice(b * QLEN + q * P, b * QLEN + (q + 1) * P), slice(b * CLEN, (b + 1) * CLEN)
                product(ring[S_BANKS[QTB * u + q]][:], [(q_hi[:, h, toks], q_lo[:, h, toks], k_hi[:, h, part], k_lo[:, h, part])]).then_inc(s_filled, 1)

            def transpose_p(j):
                u, half = divmod(j, 2)
                for t in range(2):
                    for q in range(QTB):
                        src = (2 * half + t) * P
                        last = pe.transpose(ring[PT_BANKS[j]][:, t * QLEN + q * P:t * QLEN + (q + 1) * P],
                                            probs[:, u, q, src:src + P], ident[:])
                last.then_inc(pT_filled, 1)

            def context(u):
                h, b = UNITS[u]
                cols = slice(h * HD, (h + 1) * HD)
                product(ps_ctx[:, 0:QLEN], [(v_hi[:, CTB * b + t, cols], v_lo[:, CTB * b + t, cols], pT_hi[:, t, :], pT_lo[:, t, :])
                                            for t in range(CTB)]).then_inc(o_filled, 1)

            def output(h, stop=False):
                for t in range(QT):
                    toks = slice(t * P, (t + 1) * P)
                    last = product(acc[t // 2][:, (t % 2) * D:(t % 2 + 1) * D], [(o_hi[:, h, toks], o_lo[:, h, toks], wo_hi[:, h, :], wo_lo[:, h, :])],
                                   start=False, stop=stop and t % 2 == 1)
                if stop:
                    last.then_inc(acc_filled, 1)

            def clear_acc(n):
                if n > 0:
                    pe.wait_ge(x_ready, 2 * n)
                for a in acc:
                    pe.matmul(a[:], zeros[:, 0:P], zeros[:], start=True, stop=False)

            def transpose_z(norm, where):
                pe.wait_ge(z_ready, QT * (norm + 1))
                for c in range(DC):
                    for t in range(QT):
                        last = pe.transpose(ring[H_BANKS[where][c]][:, t * P:(t + 1) * P], z_sb[:, t, c * P:(c + 1) * P], ident[:])
                    last.then_inc(h_filled, 1)

            def prologue(layer):
                first = PAIRS * layer
                pe.wait_ge(wk_split, first + 1)
                for j in range(NK):
                    project_k(j, "prologue")
                pe.wait_ge(wv_split, first + 1)
                if layer == 0:
                    pe.wait_ge(cols_copied, 2)
                project_v(0, "prologue")
                pe.wait_ge(k_split, NK * first + 1)
                project_v(1, "prologue")
                pe.wait_ge(k_split, NK * first + 2)
                project_v(2, "prologue")
                project_v(3, "prologue")
                pe.wait_ge(k_split, NK * (first + 1))
                transpose_z(layer, "prologue")
                if layer == 0:
                    pe.wait_ge(zeros_ready, 1)
                clear_acc(layer)
                pe.wait_ge(wq_split, first + 1)
                pe.wait_ge(h_split, DC * (layer + 1))
                pe.wait_ge(v_summed, NV * first + 1)
                project_q(0, "prologue")
                pe.wait_ge(v_summed, NV * first + 2)
                project_q(1, "prologue")

            def step(pair, last=False):
                nxt = pair + 1
                pe.wait_ge(q_split, NQ * nxt)
                pe.wait_ge(k_split, NK * nxt)
                scores(0, 0)
                scores(0, 1)
                pe.wait_ge(v_summed, NV * pair + 3)
                scores(1, 0)
                scores(1, 1)
                if not last:
                    pe.wait_ge(wk_split, pair + 2)
                    project_k(0, "step")
                pe.wait_ge(exp_done, NS * pair + 1)
                scores(2, 0)
                pe.wait_ge(exp_done, NS * pair + 2)
                scores(2, 1)
                pe.wait_ge(exp_done, NS * pair + 3)
                if not last:
                    project_k(1, "step")
                pe.wait_ge(exp_done, NS * pair + 4)
                pe.wait_ge(p_ready, NS * pair + 2)
                transpose_p(0)
                if not last:
                    pe.wait_ge(k_split, NK * nxt + 1)
                transpose_p(1)
                pe.wait_ge(exp_done, NS * pair + 5)
                scores(3, 0)
                pe.wait_ge(exp_done, NS * pair + 6)
                scores(3, 1)
                if not last:
                    pe.wait_ge(k_split, NK * nxt + 2)
                    pe.wait_ge(wq_split, pair + 2)
                    project_q(0, "step")
                pe.wait_ge(v_split, NV * nxt)
                pe.wait_ge(pT_split, NT * pair + 2)
                context(0)
                pe.wait_ge(p_ready, NS * pair + 4)
                transpose_p(2)
                transpose_p(3)
                if not last:
                    pe.wait_ge(exp_done, NS * pair + 7)
                    project_k(2, "step")
                    pe.wait_ge(exp_done, NS * pair + 8)
                    project_k(3, "step")
                pe.wait_ge(o_split, NU * pair + 1)
                pe.wait_ge(pT_split, NT * pair + 4)
                context(1)
                pe.wait_ge(p_ready, NS * pair + 6)
                if not last:
                    pe.wait_ge(q_split, NQ * nxt + 1)
                transpose_p(4)
                transpose_p(5)
                if not last:
                    project_q(1, "step")
                pe.wait_ge(o_split, NU * pair + 2)
                pe.wait_ge(wo_split, pair + 1)
                output(0)
                pe.wait_ge(pT_split, NT * pair + 6)
                context(2)
                pe.wait_ge(p_ready, NS * pair + 8)
                if not last:
                    pe.wait_ge(k_split, NK * nxt + 3)
                transpose_p(6)
                if not last:
                    pe.wait_ge(k_split, NK * nxt + 4)
                transpose_p(7)
                if not last:
                    pe.wait_ge(wv_split, pair + 2)
                    project_v(0, "step")
                    project_v(1, "step")
                pe.wait_ge(o_split, NU * pair + 3)
                pe.wait_ge(pT_split, NT * pair + 8)
                context(3)
                if not last:
                    pe.wait_ge(q_split, NQ * nxt + 2)
                    project_v(2, "step")
                pe.wait_ge(o_split, NU * nxt)
                if not last:
                    project_v(3, "step")
                output(1, stop=last)

            pe.wait_ge(ident_ready, 2)
            for j in range(DC * BATCH):
                b, c = divmod(j, DC)
                pe.wait_ge(c_loaded[b], LOAD)
                for t in range(CTB):
                    last = pe.transpose(ring[j][:, t * P:(t + 1) * P], c_raw[:, CTB * b + t, c * P:(c + 1) * P], ident[:])
                last.then_inc(cT_filled, 1)
            pe.wait_ge(rows_loaded, 2 * LOAD)
            pe.transpose(ring[4][:, 0:P], head_rows[:], ident[:])
            pe.transpose(ring[4][:, P:P + 20], dim_rows[:], ident[0:20, 0:20]).then_inc(cols_filled, 1)
            pe.wait_ge(cT_split, DC * BATCH)
            for layer in range(LAYERS):
                prologue(layer)
                with pe.Fori(PAIRS * layer, PAIRS * (layer + 1) - 1) as pair:
                    step(pair)
                step(PAIRS * (layer + 1) - 1, last=True)

            def hidden_layer(f):
                if f < 2:
                    w_hi, w_lo, cols = wk_hi, wk_lo, slice(f * P, (f + 1) * P)
                    pe.wait_ge(wk_split, ALL_PAIRS + 1)
                else:
                    w_hi, w_lo, cols = wf1_hi, wf1_lo, slice((f - 2) * P, (f - 1) * P)
                    pe.wait_ge(wf_split, f // 2)
                if f >= 5:
                    pe.wait_ge(gelu_done, f - 4)
                product(ring[G_BANKS[f]][:], [(w_hi[:, c, cols], w_lo[:, c, cols], h_hi[:, c, :], h_lo[:, c, :])
                                              for c in range(DC)]).then_inc(g_filled, 1)

            def mlp_output(f):
                pe.wait_ge(g_split, f + 1)
                pe.wait_ge(wf_split, 4 + f // 2)
                for t in range(QT):
                    toks = slice(t * P, (t + 1) * P)
                    last = product(acc[t // 2][:, (t % 2) * D:(t % 2 + 1) * D],
                                   [(hidden(k_hi, v_hi, f)[:, toks], hidden(k_lo, v_lo, f)[:, toks], wf2_hi[:, f, :], wf2_lo[:, f, :])],
                                   start=False, stop=f == FT - 1 and t % 2 == 1)
                return last

            clear_acc(LAYERS)
            transpose_z(LAYERS, "mlp")
            pe.wait_ge(h_split, DC * NORMS)
            for f in range(FT + 2):
                if f < FT:
                    hidden_layer(f)
                if f >= 2:
                    last = mlp_output(f - 2)
            last.then_inc(acc_filled, 1)


def kernel(**inputs):
    import numpy as np
    import concourse.bacc as bacc
    from concourse.bass_utils import run_bass_kernel_spmd

    def a(name):
        return np.asarray(inputs["L0_xattn_" + name])

    def heads(name):
        return [a(f"{name}{layer}").reshape(HEADS, HD) for layer in (1, 2)]

    arrays = {
        "x_in": np.asarray(inputs["x"]),
        "ctx_in": np.asarray(inputs["ctx_2048"]),
        "wq_in": np.concatenate([a("wq1"), a("wq2")], axis=1),
        "wk_in": np.concatenate([a("wk1"), a("wk2"), a("w_fc1")[:, :PW]], axis=1),
        "wv_in": np.concatenate([a("wv1"), a("wv2")], axis=1),
        "wo_in": np.concatenate([a("wo1"), a("wo2")], axis=0),
        "vrows_in": np.stack([np.concatenate([a("bv1"), a("bv2")]),
                              np.concatenate([a("bias_v1").ravel(), a("bias_v2").ravel()])]),
        "head_rows_in": np.concatenate(heads("bq") + heads("bk") + heads("bias_v") + heads("bias_k"), axis=0),
        "dim_rows_in": np.concatenate([a(n) for n in ("ln1_scale", "ln1_offset", "ln2_scale", "ln2_offset",
                                                      "ln_mlp_scale", "ln_mlp_offset", "b_fc1")]).reshape(20, P),
        "out_rows_in": np.stack([a("bo1"), a("bo2"), a("b_fc2")]),
        "wf1_in": np.ascontiguousarray(a("w_fc1")[:, PW:]),
        "wf2_in": a("w_fc2"),
    }
    arrays = {name: np.ascontiguousarray(v) for name, v in arrays.items()}
    nc = bacc.Bacc("TRN2", target_bir_lowering=False, num_devices=1)
    args = [nc.dram_tensor(name, v.shape, mybir.dt.from_np(v.dtype), kind="ExternalInput").ap() for name, v in arrays.items()]
    args.append(nc.dram_tensor("out", (BATCH, QLEN, D), F32, kind="ExternalOutput").ap())
    build_program(nc, *args)
    result = run_bass_kernel_spmd(nc, [arrays], core_ids=[0])
    return result.results[0]["out"]
```

```python
from contextlib import ExitStack

import concourse.bass as bass
from concourse import mybir

F32 = mybir.dt.float32
F32R = mybir.dt.float32r
ALU = mybir.AluOpType
ACT = mybir.ActivationFunctionType
AX_X = mybir.AxisListType.X

P = 128
BATCH, QLEN, CLEN, D = 2, 256, 512, 256
HEADS, HD, F = 16, 128, 1024
LAYERS = 2
LN_EPS = 1e-5
SCALE = float(HD) ** -0.5

DC = D // P
TOK = BATCH * QLEN
QT = TOK // P
QTB = QLEN // P
CT = BATCH * CLEN // P
CTB = CLEN // P
PW = 2 * HD
PAIRS = HEADS // 2
ALL_PAIRS = LAYERS * PAIRS
FT = F // P
FB = F - PW
NORMS = LAYERS + 1
UNITS = [(0, 0), (0, 1), (1, 0), (1, 1)]
NU = len(UNITS)
NS = NU * QTB
NT = NU * 2
NK = 2 * BATCH
NQ = 2
NV = CT // 2
BQ, BK, BV, BIAS_K = 0, 1, 2, 3
CTX_BANK = 5
S_BANKS = [0, 1, 2, 3, 0, 1, 0, 1]
PT_BANKS = [3, 4, 3, 4, 2, 3, 0, 1]
K_BANKS = {"step": [4, 2, 0, 1], "prologue": [0, 1, 2, 3]}
Q_BANKS = {"step": [2, 4], "prologue": [0, 3]}
V_BANKS = {"step": [2, 3, 4, CTX_BANK], "prologue": [1, 4, 1, CTX_BANK]}
H_BANKS = {"prologue": [0, 2], "mlp": [0, 1]}
G_BANKS = [(f + 2) % 5 for f in range(FT)]
BY_BATCH = 4
LOAD = 16


def build_program(nc, x_in, ctx_in, wq_in, wk_in, wv_in, wo_in, vrows_in, head_rows_in,
                  dim_rows_in, out_rows_in, wf1_in, wf2_in, out):
    with ExitStack() as stack:
        def sb(name, shape, dt=F32):
            return stack.enter_context(nc.sbuf_tensor(name, shape, dt))

        def sem(name):
            return stack.enter_context(nc.semaphore(name))

        ring = [stack.enter_context(nc.psum_tensor(f"ring{i}", [P, 512], F32)) for i in range(5)]
        ring.append(stack.enter_context(nc.psum_tensor("ps_ctx", [P, 512], F32)))
        ps_ctx = ring[CTX_BANK]
        acc = [stack.enter_context(nc.psum_tensor(f"acc{i}", [P, 512], F32)) for i in range(2)]

        ident = sb("ident", [P, P])
        zeros = sb("zeros", [P, 512], F32R)
        minus_half = sb("minus_half", [P, QT])
        head_rows = sb("head_rows", [P, P])
        dim_rows = sb("dim_rows", [20, P])
        head_cols = sb("head_cols", [P, 4, LAYERS * HEADS])
        step_cols = sb("step_cols", [P, ALL_PAIRS + 1, 3, 2])
        cols = sb("cols", [P, 3, 2])
        dim_cols = sb("dim_cols", [P, 20])
        out_rows = sb("out_rows", [P, NORMS, D])
        cT_hi = sb("cT_hi", [P, DC, CT * P], F32R)
        cT_lo = sb("cT_lo", [P, DC, CT * P], F32R)
        x_sb = sb("x_sb", [P, QT, D])
        x_res = sb("x_res", [P, QT, D])
        z_sb = sb("z_sb", [P, QT, D])
        h_full = sb("h_full", [P, DC, TOK])
        h_hi = sb("h_hi", [P, DC, TOK], F32R)
        h_lo = sb("h_lo", [P, DC, TOK], F32R)
        bn = sb("bn", [P, QT, 6])
        mean_var = sb("mean_var", [P, QT, 2])
        var_eps = sb("var_eps", [P, QT])
        rstd = sb("rstd", [P, QT])
        wq_raw = sb("wq_raw", [P, DC, PW])
        wk_raw = sb("wk_raw", [P, DC, PW])
        wv_raw = sb("wv_raw", [P, DC, PW])
        wo_raw = sb("wo_raw", [P, 2, D])
        wq_hi, wq_lo = sb("wq_hi", [P, DC, PW], F32R), sb("wq_lo", [P, DC, PW], F32R)
        wk_hi, wk_lo = sb("wk_hi", [P, DC, PW], F32R), sb("wk_lo", [P, DC, PW], F32R)
        wv_hi, wv_lo = sb("wv_hi", [P, DC, PW], F32R), sb("wv_lo", [P, DC, PW], F32R)
        wo_hi, wo_lo = sb("wo_hi", [P, 2, D], F32R), sb("wo_lo", [P, 2, D], F32R)
        vrows = sb("vrows", [P, 2, PW])
        vbias = sb("vbias", [P, PW])
        q_hi, q_lo = sb("q_hi", [P, 2, TOK], F32R), sb("q_lo", [P, 2, TOK], F32R)
        k_hi, k_lo = sb("k_hi", [P, 2, CT * P], F32R), sb("k_lo", [P, 2, CT * P], F32R)
        v_sum = sb("v_sum", [P, 2, 2 * PW])
        v_hi, v_lo = sb("v_hi", [P, CT, PW], F32R), sb("v_lo", [P, CT, PW], F32R)
        probs = sb("probs", [P, NU, QTB, CLEN])
        row_max = sb("row_max", [P, NU, QTB])
        shift = sb("shift", [P, NU, QTB])
        p_learned = sb("p_learned", [P, NU, QTB])
        row_sum = sb("row_sum", [P, NU, QTB])
        total = sb("total", [P, NU, QTB])
        inv = sb("inv", [P, NU, QTB])
        pT_hi, pT_lo = sb("pT_hi", [P, CTB, QLEN], F32R), sb("pT_lo", [P, CTB, QLEN], F32R)
        o_hi, o_lo = sb("o_hi", [P, 2, TOK], F32R), sb("o_lo", [P, 2, TOK], F32R)
        wf_raw = sb("wf_raw", [P, 2, 512])
        wf1_hi, wf1_lo = sb("wf1_hi", [P, DC, FB], F32R), sb("wf1_lo", [P, DC, FB], F32R)
        wf2_hi, wf2_lo = sb("wf2_hi", [P, FT, D], F32R), sb("wf2_lo", [P, FT, D], F32R)

        g_full = v_sum
        c_raw = probs[:].rearrange("p u q t -> p (u q t)")[:, 0:CT * D].rearrange("p (t d) -> p t d", d=D)

        def hidden(part_k, part_v, f):
            if f < FT // 2:
                return part_k[:].rearrange("p h t -> p (h t)")[:, f * 512:(f + 1) * 512]
            return part_v[:].rearrange("p t c -> p (t c)")[:, (f - FT // 2) * 512:(f - FT // 2 + 1) * 512]

        c_loaded = [sem(f"c_loaded{b}") for b in range(BATCH)]
        x_loaded, rows_loaded, out_rows_loaded = sem("x_loaded"), sem("rows_loaded"), sem("out_rows_loaded")
        wq_loaded, wk_loaded, wv_loaded, wo_loaded = (sem(f"w{n}_loaded") for n in "qkvo")
        wq_split, wk_split, wv_split, wo_split = (sem(f"w{n}_split") for n in "qkvo")
        wq_rounded, wk_rounded, wv_rounded, wo_rounded = (sem(f"w{n}_rounded") for n in "qkvo")
        wf_loaded = [sem(f"wf_loaded{i}") for i in range(2)]
        wf_rounded, wf_split = sem("wf_rounded"), sem("wf_split")
        ident_ready, zeros_ready = sem("ident_ready"), sem("zeros_ready")
        cT_filled, cT_rounded, cT_split = sem("cT_filled"), sem("cT_rounded"), sem("cT_split")
        cols_filled, cols_copied, cols_ready = sem("cols_filled"), sem("cols_copied"), sem("cols_ready")
        x_ready, bn_done, stats_ready = sem("x_ready"), sem("bn_done"), sem("stats_ready")
        eps_added, rstd_ready, z_ready = sem("eps_added"), sem("rstd_ready"), sem("z_ready")
        h_filled, h_drained, h_rounded, h_split = (sem(f"h_{n}") for n in ("filled", "drained", "rounded", "split"))
        res_ready = sem("res_ready")
        k_filled, k_rounded, k_split = sem("k_filled"), sem("k_rounded"), sem("k_split")
        q_filled, q_rounded, q_split = sem("q_filled"), sem("q_rounded"), sem("q_split")
        v_filled, v_summed, v_rounded, v_split = (sem(f"v_{n}") for n in ("filled", "summed", "rounded", "split"))
        s_filled, max_done, shift_ready = sem("s_filled"), sem("max_done"), sem("shift_ready")
        exp_done, total_done, inv_ready, p_ready = sem("exp_done"), sem("total_done"), sem("inv_ready"), sem("p_ready")
        pT_filled, pT_rounded, pT_split = sem("pT_filled"), sem("pT_rounded"), sem("pT_split")
        o_filled, o_rounded, o_split = sem("o_filled"), sem("o_rounded"), sem("o_split")
        acc_filled = sem("acc_filled")
        g_filled, gelu_done, g_rounded, g_split = (sem(f"g_{n}") for n in ("filled", "gelu", "rounded", "split"))
        passed, stored = sem("passed"), sem("stored")

        block = stack.enter_context(nc.Block())

        @block.sync
        def _(sp):
            def load_wk(n):
                sp.dma_start(wk_raw[:], wk_in[:, bass.ds(n * PW, PW)].rearrange("(c p) n -> p c n", p=P)).then_inc(wk_loaded, LOAD)

            def load_wq(n):
                sp.dma_start(wq_raw[:], wq_in[:, bass.ds(n * PW, PW)].rearrange("(c p) n -> p c n", p=P)).then_inc(wq_loaded, LOAD)

            def load_wv(n):
                sp.dma_start(wv_raw[:], wv_in[:, bass.ds(n * PW, PW)].rearrange("(c p) n -> p c n", p=P)).then_inc(wv_loaded, LOAD)
                sp.dma_start(vrows[:], vrows_in[:, bass.ds(n * PW, PW)].rearrange("(o r) n -> o r n", o=1).to_broadcast([P, 2, PW])).then_inc(wv_loaded, LOAD)

            def load_wo(n):
                sp.dma_start(wo_raw[:], wo_in[bass.ds(n * PW, PW), :].rearrange("(h p) n -> p h n", p=P)).then_inc(wo_loaded, LOAD)

            c_view = ctx_in.rearrange("b (t p) d -> p (b t) d", p=P)
            for b in range(BATCH):
                tiles = slice(CTB * b, CTB * (b + 1))
                sp.dma_start(c_raw[:, tiles, :], c_view[:, tiles, :]).then_inc(c_loaded[b], LOAD)
                if b == 0:
                    load_wk(0)
            sp.dma_start(head_rows[:], head_rows_in).then_inc(rows_loaded, LOAD)
            sp.dma_start(dim_rows[:], dim_rows_in).then_inc(rows_loaded, LOAD)
            sp.dma_start(x_sb[:], x_in.rearrange("b (t p) d -> p (b t) d", p=P)).then_inc(x_loaded, LOAD)
            load_wv(0)
            load_wq(0)
            load_wo(0)
            sp.dma_start(out_rows[:], out_rows_in.rearrange("(o r) n -> o r n", o=1).to_broadcast([P, NORMS, D])).then_inc(out_rows_loaded, LOAD)
            sp.wait_ge(wk_split, 1)
            load_wk(1)
            sp.wait_ge(wv_split, 1)
            load_wv(1)
            sp.wait_ge(wq_split, 1)
            load_wq(1)
            sp.wait_ge(wk_split, 2)
            load_wk(2)

            def refill(pair, wq=True, wk=True):
                if wq:
                    sp.wait_ge(wq_split, pair + 2)
                    load_wq(pair + 2)
                    sp.wait_ge(wv_split, pair + 2)
                    load_wv(pair + 2)
                sp.wait_ge(wo_split, pair + 1)
                load_wo(pair + 1)
                if wk:
                    sp.wait_ge(wk_split, pair + 3)
                    load_wk(pair + 3)

            def load_mlp(part):
                if part < 3:
                    src = wf1_in[:, PW * part:PW * (part + 1)].rearrange("(c p) n -> p c n", p=P)
                    dst = wf_raw[:, part % 2, :].rearrange("p (c n) -> p c n", c=DC)
                else:
                    src = wf2_in[PW * (part - 3):PW * (part - 2), :].rearrange("(f p) n -> p f n", p=P)
                    dst = wf_raw[:, part % 2, :].rearrange("p (f n) -> p f n", n=D)
                if part >= 2:
                    sp.wait_ge(wf_split, part - 1)
                sp.dma_start(dst, src).then_inc(wf_loaded[part % 2], LOAD)

            load_mlp(0)
            load_mlp(1)
            with sp.Fori(0, PAIRS - 1) as pair:
                refill(pair)
            refill(PAIRS - 1)
            for part in range(2, 5):
                load_mlp(part)
            with sp.Fori(PAIRS, ALL_PAIRS - 2) as pair:
                refill(pair)
            refill(ALL_PAIRS - 2, wq=False, wk=False)
            for part in range(5, 7):
                load_mlp(part)

            for t in range(QT):
                if t % 2 == 0:
                    sp.wait_ge(x_ready, 2 * LAYERS + 1 + t // 2)
                sp.dma_start(out.rearrange("b (t p) d -> p (b t) d", p=P)[:, t, :], x_sb[:, t, :]).then_inc(stored, LOAD)
            sp.wait_ge(stored, QT * LOAD)

        @block.gpsimd
        def _(pool):
            def hold(semaphore, value):
                pool.wait_ge(semaphore, value)
                pool.sem_inc(passed, 1)

            def split_tile(raw, hi, lo, rounded, n, done):
                pool.tensor_scalar(hi, raw, 1.0, 0.0, ALU.mult, ALU.add).then_inc(rounded, 1)
                pool.wait_ge(rounded, n)
                pool.tensor_tensor(lo, raw, hi.bitcast(F32), ALU.subtract).then_inc(done, 1)

            def split_wk(n):
                hold(wk_loaded, (n + 1) * LOAD)
                split_tile(wk_raw[:], wk_hi[:], wk_lo[:], wk_rounded, n + 1, wk_split)

            def split_wq(n):
                hold(wq_loaded, (n + 1) * LOAD)
                split_tile(wq_raw[:], wq_hi[:], wq_lo[:], wq_rounded, n + 1, wq_split)

            def split_wv(n):
                pool.wait_ge(wv_loaded, (2 * n + 2) * LOAD)
                pool.tensor_tensor(vbias[:], vrows[:, 0, :], vrows[:, 1, :], ALU.subtract)
                split_tile(wv_raw[:], wv_hi[:], wv_lo[:], wv_rounded, n + 1, wv_split)

            def split_wo(n):
                hold(wo_loaded, (n + 1) * LOAD)
                split_tile(wo_raw[:], wo_hi[:], wo_lo[:], wo_rounded, n + 1, wo_split)

            def split_mlp(part):
                pool.wait_ge(wf_loaded[part % 2], (part // 2 + 1) * LOAD)
                if part < 3:
                    hi = wf1_hi[:, :, PW * part:PW * (part + 1)]
                    lo = wf1_lo[:, :, PW * part:PW * (part + 1)]
                    raw = wf_raw[:, part % 2, :].rearrange("p (c n) -> p c n", c=DC)
                else:
                    f = 2 * (part - 3)
                    hi, lo = wf2_hi[:, f:f + 2, :], wf2_lo[:, f:f + 2, :]
                    raw = wf_raw[:, part % 2, :].rearrange("p (f n) -> p f n", n=D)
                split_tile(raw, hi, lo, wf_rounded, part + 1, wf_split)

            def inverse_deviation(norm, b):
                tiles = slice(QTB * b, QTB * (b + 1))
                half = BATCH * norm + b + 1
                pool.wait_ge(stats_ready, half)
                pool.tensor_scalar(var_eps[:, tiles], mean_var[:, tiles, 1], 1.0, LN_EPS, ALU.mult, ALU.add).then_inc(eps_added, 1)
                pool.wait_ge(eps_added, half)
                pool.tensor_tensor(rstd[:, tiles], var_eps[:, tiles], minus_half[:, tiles], ALU.pow).then_inc(rstd_ready, 1)

            def residual(norm):
                rows = out_rows[:, norm:norm + 1, :].to_broadcast([P, QT, D])
                pool.tensor_tensor(x_res[:], x_sb[:], rows, ALU.add).then_inc(res_ready, 1)

            def value_rest(pair, m):
                pool.wait_ge(v_rounded, NV * pair + m + 1)
                pool.tensor_tensor(v_lo[:, 2 * m:2 * m + 2, :], v_sum[:, m % 2, :].rearrange("p (t c) -> p t c", c=PW),
                                   v_hi[:, 2 * m:2 * m + 2, :].bitcast(F32), ALU.subtract).then_inc(v_split, 1)

            def normalise(pair, u):
                hold(inv_ready, NU * pair + u + 1)
                for q in range(QTB):
                    pool.tensor_scalar(probs[:, u, q, :], probs[:, u, q, :], inv[:, u, q:q + 1], 0.0, ALU.mult, ALU.add).then_inc(p_ready, 1)

            pool.memset(ident[:], 0.0).then_inc(ident_ready, 1)
            pool.memset(minus_half[:], -0.5)
            pool.wait_ge(ident_ready, 1)
            pool.affine_select(out=ident[:], in_=ident[:], compare_op=ALU.not_equal, fill=1.0, base=0,
                               pattern=[[-1, P]], channel_multiplier=1).then_inc(ident_ready, 1)
            pool.memset(zeros[:].bitcast(F32), 0.0).then_inc(zeros_ready, 1)
            split_wk(0)
            pool.wait_ge(cols_copied, 2)
            by_pair = head_cols[:].rearrange("p g (n h) -> p g n h", h=2)
            pool.memset(step_cols[:, 0, BV, :], 0.0)
            pool.memset(step_cols[:, ALL_PAIRS, 0:2, :], 0.0)
            pool.tensor_tensor(step_cols[:, 0:ALL_PAIRS, BK, :], by_pair[:, BK], by_pair[:, BIAS_K], ALU.subtract)
            pool.tensor_copy(step_cols[:, 0:ALL_PAIRS, BQ, :], by_pair[:, BQ])
            pool.tensor_copy(step_cols[:, 1:ALL_PAIRS + 1, BV, :], by_pair[:, BV]).then_inc(cols_ready, 1)

            def prologue(layer):
                first = PAIRS * layer
                if layer == 0:
                    split_wv(0)
                for b in range(BATCH):
                    inverse_deviation(layer, b)
                if layer == 0:
                    split_wq(0)
                    pool.wait_ge(k_filled, NK)
                    split_wk(1)
                for m in range(NV):
                    value_rest(first, m)

            def step(pair, last=False, final=False):
                if not final:
                    pool.wait_ge(q_filled, NQ * (pair + 1))
                    split_wq(pair + 1)
                normalise(pair, 0)
                normalise(pair, 1)
                if not final:
                    pool.wait_ge(v_summed, NV * (pair + 1))
                    split_wv(pair + 1)
                normalise(pair, 2)
                pool.wait_ge(s_filled, NS * pair + 1)
                split_wo(pair)
                normalise(pair, 3)
                if not final:
                    pool.wait_ge(k_filled, NK * (pair + 2))
                    split_wk(pair + 2)
                if not last:
                    for m in range(NV):
                        value_rest(pair + 1, m)

            prologue(0)
            with pool.Fori(0, PAIRS - 1) as pair:
                step(pair)
            step(PAIRS - 1, last=True)
            pool.wait_ge(out_rows_loaded, LOAD)
            residual(0)
            for part in range(3):
                split_mlp(part)
            prologue(1)
            with pool.Fori(PAIRS, ALL_PAIRS - 1) as pair:
                step(pair)
            step(ALL_PAIRS - 1, last=True, final=True)
            residual(1)
            for part in range(3, 6):
                split_mlp(part)
            for b in range(BATCH):
                inverse_deviation(LAYERS, b)
            split_mlp(6)
            residual(LAYERS)

        @block.scalar
        def _(act):
            def column(group, pair, h, where):
                return cols[:, group, h:h + 1] if where == "step" else step_cols[:, pair, group, h:h + 1]

            def round_k(pair, j, where):
                h, b = divmod(j, BATCH)
                act.wait_ge(k_filled, NK * pair + j + 1)
                act.activation(k_hi[:, h, b * CLEN:(b + 1) * CLEN], ring[K_BANKS[where][j]][:], ACT.Identity,
                               bias=column(BK, pair, h, where)).then_inc(k_rounded, 1)

            def round_q(pair, h, where):
                act.wait_ge(q_filled, NQ * pair + h + 1)
                act.activation(q_hi[:, h, :], ring[Q_BANKS[where][h]][:], ACT.Identity,
                               bias=column(BQ, pair, h, where)).then_inc(q_rounded, 1)

            def round_v(pair, m):
                act.wait_ge(v_summed, NV * pair + m + 1)
                act.activation(v_hi[:, 2 * m:2 * m + 2, :], v_sum[:, m % 2, :].rearrange("p (t c) -> p t c", c=PW),
                               ACT.Copy).then_inc(v_rounded, 1)

            def round_pT(pair, j):
                half = j % 2
                act.wait_ge(pT_filled, NT * pair + j + 1)
                act.activation(pT_hi[:, 2 * half:2 * half + 2, :], ring[PT_BANKS[j]][:].rearrange("p (t q) -> p t q", q=QLEN),
                               ACT.Copy).then_inc(pT_rounded, 1)

            def round_o(pair, u):
                h, b = UNITS[u]
                act.wait_ge(o_filled, NU * pair + u + 1)
                act.activation(o_hi[:, h, b * QLEN:(b + 1) * QLEN], ps_ctx[:, 0:QLEN], ACT.Identity,
                               bias=cols[:, BV, h:h + 1]).then_inc(o_rounded, 1)

            def exponentials(pair, u):
                act.wait_ge(shift_ready, NU * pair + u + 1)
                act.activation(p_learned[:, u, :], shift[:, u, :], ACT.Exp)
                for q in range(QTB):
                    act.activation(probs[:, u, q, :], ring[S_BANKS[QTB * u + q]][:], ACT.Exp, bias=shift[:, u, q:q + 1],
                                   scale=SCALE, accum_out=row_sum[:, u, q:q + 1]).then_inc(exp_done, 1)

            def round_h(norm, b):
                act.wait_ge(h_drained, DC * (BATCH * norm + b + 1))
                act.activation(h_hi[:, :, b * QLEN:(b + 1) * QLEN], h_full[:, :, b * QLEN:(b + 1) * QLEN], ACT.Copy).then_inc(h_rounded, 1)

            def prologue(layer):
                first = PAIRS * layer
                if layer == 0:
                    for j in range(NK):
                        round_k(first, j, "prologue")
                round_h(layer, 0)
                round_v(first, 0)
                round_h(layer, 1)
                round_v(first, 1)
                round_v(first, 2)
                for h in range(NQ):
                    round_q(first, h, "prologue")
                round_v(first, 3)

            def step(pair, last=False, final=False):
                exponentials(pair, 0)
                exponentials(pair, 1)
                if not final:
                    round_k(pair + 1, 0, "step")
                exponentials(pair, 2)
                if not final:
                    round_k(pair + 1, 1, "step")
                round_pT(pair, 0)
                round_pT(pair, 1)
                if not last:
                    round_q(pair + 1, 0, "step")
                exponentials(pair, 3)
                round_o(pair, 0)
                round_pT(pair, 2)
                round_pT(pair, 3)
                if not final:
                    round_k(pair + 1, 2, "step")
                    round_k(pair + 1, 3, "step")
                round_o(pair, 1)
                round_pT(pair, 4)
                round_pT(pair, 5)
                if not last:
                    round_q(pair + 1, 1, "step")
                round_o(pair, 2)
                round_pT(pair, 6)
                round_pT(pair, 7)
                if not last:
                    round_v(pair + 1, 0)
                    round_v(pair + 1, 1)
                round_o(pair, 3)
                if not last:
                    round_v(pair + 1, 2)
                    round_v(pair + 1, 3)

            for j in range(DC * BATCH):
                b, c = divmod(j, DC)
                act.wait_ge(cT_filled, j + 1)
                act.activation(cT_hi[:, c, b * CLEN:(b + 1) * CLEN], ring[j][:], ACT.Copy).then_inc(cT_rounded, 1)
            act.wait_ge(cols_ready, 1)
            for layer in range(LAYERS):
                prologue(layer)
                with act.Fori(PAIRS * layer, PAIRS * (layer + 1) - 1) as pair:
                    step(pair)
                step(PAIRS * (layer + 1) - 1, last=True, final=layer == LAYERS - 1)
            for b in range(BATCH):
                round_h(LAYERS, b)
            for f in range(FT):
                act.wait_ge(g_filled, f + 1)
                if f >= 2:
                    act.wait_ge(g_split, f - 1)
                act.activation(g_full[:, f % 2, :], ring[G_BANKS[f]][:], ACT.Gelu,
                               bias=dim_cols[:, 4 * NORMS + f:4 * NORMS + f + 1]).then_inc(gelu_done, 1)

        @block.vector
        def _(dve):
            def column(group, pair, h, where):
                return cols[:, group, h:h + 1] if where == "step" else step_cols[:, pair, group, h:h + 1]

            def split_k(pair, j, where):
                h, b = divmod(j, BATCH)
                part = slice(b * CLEN, (b + 1) * CLEN)
                dve.wait_ge(k_rounded, NK * pair + j + 1)
                dve.scalar_tensor_tensor(out=k_lo[:, h, part], in0=ring[K_BANKS[where][j]][:],
                                         scalar=column(BK, pair, h, where),
                                         in1=k_hi[:, h, part].bitcast(F32), op0=ALU.add, op1=ALU.subtract).then_inc(k_split, 1)

            def split_q(pair, h, where):
                dve.wait_ge(q_rounded, NQ * pair + h + 1)
                dve.scalar_tensor_tensor(out=q_lo[:, h, :], in0=ring[Q_BANKS[where][h]][:],
                                         scalar=column(BQ, pair, h, where),
                                         in1=q_hi[:, h, :].bitcast(F32), op0=ALU.add, op1=ALU.subtract).then_inc(q_split, 1)

            def sum_v(pair, m, where):
                dve.wait_ge(v_filled, NV * pair + m + 1)
                if not isinstance(pair, int) or NV * pair + m >= 2:
                    dve.wait_ge(v_split, NV * pair + m - 1)
                dve.tensor_tensor(v_sum[:, m % 2, :].rearrange("p (t c) -> p t c", c=PW),
                                  ring[V_BANKS[where][m]][:].rearrange("p (t c) -> p t c", c=PW),
                                  vbias[:].rearrange("p (o c) -> p o c", o=1).to_broadcast([P, 2, PW]), ALU.add).then_inc(v_summed, 1)

            def split_pT(pair, j):
                half = j % 2
                dve.wait_ge(pT_rounded, NT * pair + j + 1)
                dve.tensor_tensor(pT_lo[:, 2 * half:2 * half + 2, :], ring[PT_BANKS[j]][:].rearrange("p (t q) -> p t q", q=QLEN),
                                  pT_hi[:, 2 * half:2 * half + 2, :].bitcast(F32), ALU.subtract).then_inc(pT_split, 1)

            def split_o(pair, u):
                h, b = UNITS[u]
                part = slice(b * QLEN, (b + 1) * QLEN)
                dve.wait_ge(o_rounded, NU * pair + u + 1)
                dve.scalar_tensor_tensor(out=o_lo[:, h, part], in0=ps_ctx[:, 0:QLEN],
                                         scalar=cols[:, BV, h:h + 1],
                                         in1=o_hi[:, h, part].bitcast(F32), op0=ALU.add, op1=ALU.subtract).then_inc(o_split, 1)

            def maxima(pair, u):
                for q in range(QTB):
                    dve.wait_ge(s_filled, NS * pair + QTB * u + q + 1)
                    dve.reduce_max(row_max[:, u, q:q + 1], ring[S_BANKS[QTB * u + q]][:], AX_X).then_inc(max_done, 1)
                dve.wait_ge(max_done, NS * pair + QTB * (u + 1))
                dve.tensor_scalar(shift[:, u, :], row_max[:, u, :], -SCALE, 0.0, ALU.mult, ALU.min).then_inc(shift_ready, 1)

            def inverse_sums(pair, u):
                dve.wait_ge(exp_done, NS * pair + QTB * (u + 1))
                dve.tensor_tensor(total[:, u, :], row_sum[:, u, :], p_learned[:, u, :], ALU.add).then_inc(total_done, 1)
                dve.wait_ge(total_done, NU * pair + u + 1)
                dve.reciprocal(inv[:, u, :], total[:, u, :]).then_inc(inv_ready, 1)

            def new_x(n, b):
                dve.wait_ge(acc_filled, BATCH * n + b + 1)
                dve.wait_ge(res_ready, n + 1)
                dve.tensor_tensor(x_sb[:, QTB * b:QTB * (b + 1), :], acc[b][:].rearrange("p (t d) -> p t d", d=D),
                                  x_res[:, QTB * b:QTB * (b + 1), :], ALU.add).then_inc(x_ready, 1)

            def stats(norm, b):
                if norm > 0:
                    dve.wait_ge(x_ready, BATCH * (norm - 1) + b + 1)
                for t in range(QTB * b, QTB * (b + 1)):
                    dve.bn_stats(bn[:, t, :], x_sb[:, t, :]).then_inc(bn_done, 1)
                dve.wait_ge(bn_done, QT * norm + QTB * (b + 1))
                for t in range(QTB * b, QTB * (b + 1)):
                    agg = dve.bn_aggr(mean_var[:, t, :], bn[:, t, :])
                agg.then_inc(stats_ready, 1)

            def standardise(norm, b):
                dve.wait_ge(stats_ready, BATCH * norm + b + 1)
                dve.wait_ge(rstd_ready, BATCH * norm + b + 1)
                for t in range(QTB * b, QTB * (b + 1)):
                    dve.tensor_scalar(z_sb[:, t, :], x_sb[:, t, :], mean_var[:, t, 0:1], rstd[:, t:t + 1],
                                      ALU.subtract, ALU.mult).then_inc(z_ready, 1)

            def scale_h(norm, b, where):
                dve.wait_ge(h_filled, BATCH * norm + b + 1)
                for c in range(DC):
                    dve.tensor_scalar(h_full[:, c, b * QLEN:(b + 1) * QLEN], ring[H_BANKS[where][b]][:, c * QLEN:(c + 1) * QLEN],
                                      dim_cols[:, 4 * norm + c:4 * norm + c + 1],
                                      dim_cols[:, 4 * norm + DC + c:4 * norm + DC + c + 1], ALU.mult, ALU.add).then_inc(h_drained, 1)

            def split_h(norm, b):
                part = slice(b * QLEN, (b + 1) * QLEN)
                dve.wait_ge(h_rounded, BATCH * norm + b + 1)
                dve.tensor_tensor(h_lo[:, :, part], h_full[:, :, part], h_hi[:, :, part].bitcast(F32), ALU.subtract).then_inc(h_split, 1)

            def prologue(layer):
                first = PAIRS * layer
                if layer == 0:
                    dve.wait_ge(x_loaded, LOAD)
                    stats(0, 0)
                    stats(0, 1)
                    split_k(first, 0, "prologue")
                    standardise(0, 0)
                    split_k(first, 1, "prologue")
                    standardise(0, 1)
                    split_k(first, 2, "prologue")
                    split_k(first, 3, "prologue")
                    scale_h(0, 0, "prologue")
                else:
                    standardise(layer, 0)
                    new_x(layer - 1, 1)
                    stats(layer, 1)
                    scale_h(layer, 0, "prologue")
                    standardise(layer, 1)
                split_h(layer, 0)
                dve.wait_ge(wv_split, first + 1)
                sum_v(first, 0, "prologue")
                scale_h(layer, 1, "prologue")
                sum_v(first, 1, "prologue")
                split_h(layer, 1)
                sum_v(first, 2, "prologue")
                for h in range(NQ):
                    split_q(first, h, "prologue")
                sum_v(first, 3, "prologue")

            def step(pair, last=False, final=False):
                dve.tensor_copy(cols[:].rearrange("p g h -> p (g h)"),
                                step_cols[:, bass.ds(pair + 1, 1), :, :].rearrange("p n g h -> p (n g h)"))
                maxima(pair, 0)
                maxima(pair, 1)
                inverse_sums(pair, 0)
                maxima(pair, 2)
                if not final:
                    split_k(pair + 1, 0, "step")
                inverse_sums(pair, 1)
                inverse_sums(pair, 2)
                if not final:
                    split_k(pair + 1, 1, "step")
                split_pT(pair, 0)
                split_pT(pair, 1)
                maxima(pair, 3)
                if not last:
                    split_q(pair + 1, 0, "step")
                split_o(pair, 0)
                inverse_sums(pair, 3)
                split_pT(pair, 2)
                split_pT(pair, 3)
                if not final:
                    split_k(pair + 1, 2, "step")
                    split_k(pair + 1, 3, "step")
                split_o(pair, 1)
                split_pT(pair, 4)
                split_pT(pair, 5)
                if not last:
                    split_q(pair + 1, 1, "step")
                split_o(pair, 2)
                split_pT(pair, 6)
                split_pT(pair, 7)
                if not last:
                    dve.wait_ge(wv_split, pair + 2)
                    sum_v(pair + 1, 0, "step")
                    sum_v(pair + 1, 1, "step")
                else:
                    new_x((pair + 1) // PAIRS - 1, 0)
                    stats((pair + 1) // PAIRS, 0)
                split_o(pair, 3)
                if not last:
                    sum_v(pair + 1, 2, "step")
                    sum_v(pair + 1, 3, "step")

            for j in range(DC * BATCH):
                b, c = divmod(j, DC)
                part = slice(b * CLEN, (b + 1) * CLEN)
                dve.wait_ge(cT_rounded, j + 1)
                dve.tensor_tensor(cT_lo[:, c, part], ring[j][:], cT_hi[:, c, part].bitcast(F32), ALU.subtract).then_inc(cT_split, 1)
            dve.wait_ge(cols_filled, 1)
            dve.tensor_copy(head_cols[:].rearrange("p g c -> p (g c)"), ring[4][:, 0:P]).then_inc(cols_copied, 1)
            dve.tensor_copy(dim_cols[:], ring[4][:, P:P + 20]).then_inc(cols_copied, 1)
            dve.wait_ge(cols_ready, 1)
            for layer in range(LAYERS):
                prologue(layer)
                with dve.Fori(PAIRS * layer, PAIRS * (layer + 1) - 1) as pair:
                    step(pair)
                step(PAIRS * (layer + 1) - 1, last=True, final=layer == LAYERS - 1)
            standardise(LAYERS, 0)
            new_x(LAYERS - 1, 1)
            stats(LAYERS, 1)
            scale_h(LAYERS, 0, "mlp")
            standardise(LAYERS, 1)
            split_h(LAYERS, 0)
            scale_h(LAYERS, 1, "mlp")
            split_h(LAYERS, 1)
            for f in range(FT):
                dve.wait_ge(gelu_done, f + 1)
                dve.tensor_copy(hidden(k_hi, v_hi, f), g_full[:, f % 2, :]).then_inc(g_rounded, 1)
                dve.wait_ge(g_rounded, f + 1)
                dve.tensor_tensor(hidden(k_lo, v_lo, f), g_full[:, f % 2, :], hidden(k_hi, v_hi, f).bitcast(F32),
                                  ALU.subtract).then_inc(g_split, 1)
            for b in range(BATCH):
                new_x(LAYERS, b)

        @block.tensor
        def _(pe):
            def product(out_ap, terms, start=True, stop=True):
                passes = [(a, b) for lhs_hi, lhs_lo, rhs_hi, rhs_lo in terms
                          for a, b in ((lhs_hi, rhs_lo), (lhs_lo, rhs_hi), (lhs_hi, rhs_hi))]
                for i, (a, b) in enumerate(passes):
                    ins = pe.matmul(out_ap, a, b, start=start and i == 0, stop=stop and i == len(passes) - 1)
                return ins

            def project_k(j, where):
                h, b = divmod(j, BATCH)
                cols, part = slice(h * HD, (h + 1) * HD), slice(b * CLEN, (b + 1) * CLEN)
                product(ring[K_BANKS[where][j]][:], [(wk_hi[:, c, cols], wk_lo[:, c, cols], cT_hi[:, c, part], cT_lo[:, c, part])
                                                     for c in range(DC)]).then_inc(k_filled, 1)

            def project_q(h, where, b=None):
                cols = slice(h * HD, (h + 1) * HD)
                part = slice(0, TOK) if b is None else slice(b * QLEN, (b + 1) * QLEN)
                last = product(ring[Q_BANKS[where][h]][:, part], [(wq_hi[:, c, cols], wq_lo[:, c, cols], h_hi[:, c, part], h_lo[:, c, part])
                                                                  for c in range(DC)])
                if b != 0:
                    last.then_inc(q_filled, 1)

            def project_v(m, where):
                for i in range(2):
                    toks = slice((2 * m + i) * P, (2 * m + i + 1) * P)
                    last = product(ring[V_BANKS[where][m]][:, i * PW:(i + 1) * PW],
                                   [(cT_hi[:, c, toks], cT_lo[:, c, toks], wv_hi[:, c, :], wv_lo[:, c, :]) for c in range(DC)])
                last.then_inc(v_filled, 1)

            def scores(u, q):
                h, b = UNITS[u]
                toks, part = slice(b * QLEN + q * P, b * QLEN + (q + 1) * P), slice(b * CLEN, (b + 1) * CLEN)
                product(ring[S_BANKS[QTB * u + q]][:], [(q_hi[:, h, toks], q_lo[:, h, toks], k_hi[:, h, part], k_lo[:, h, part])]).then_inc(s_filled, 1)

            def transpose_p(j):
                u, half = divmod(j, 2)
                for t in range(2):
                    for q in range(QTB):
                        src = (2 * half + t) * P
                        last = pe.transpose(ring[PT_BANKS[j]][:, t * QLEN + q * P:t * QLEN + (q + 1) * P],
                                            probs[:, u, q, src:src + P], ident[:])
                last.then_inc(pT_filled, 1)

            def context(u):
                h, b = UNITS[u]
                cols = slice(h * HD, (h + 1) * HD)
                product(ps_ctx[:, 0:QLEN], [(v_hi[:, CTB * b + t, cols], v_lo[:, CTB * b + t, cols], pT_hi[:, t, :], pT_lo[:, t, :])
                                            for t in range(CTB)]).then_inc(o_filled, 1)

            def output(h, batches=range(BATCH), stop=False):
                for b in batches:
                    for t in range(QTB):
                        toks = slice(b * QLEN + t * P, b * QLEN + (t + 1) * P)
                        last = product(acc[b][:, t * D:(t + 1) * D], [(o_hi[:, h, toks], o_lo[:, h, toks], wo_hi[:, h, :], wo_lo[:, h, :])],
                                       start=False, stop=stop and t == QTB - 1)
                    if stop:
                        last.then_inc(acc_filled, 1)

            def clear_acc(n):
                for b in range(BATCH):
                    if n > 0:
                        pe.wait_ge(x_ready, BATCH * (n - 1) + b + 1)
                    pe.matmul(acc[b][:], zeros[:, 0:P], zeros[:], start=True, stop=False)

            def transpose_z(norm, b, where):
                pe.wait_ge(z_ready, QT * norm + QTB * (b + 1))
                for c in range(DC):
                    for t in range(QTB):
                        last = pe.transpose(ring[H_BANKS[where][b]][:, c * QLEN + t * P:c * QLEN + (t + 1) * P],
                                            z_sb[:, QTB * b + t, c * P:(c + 1) * P], ident[:])
                last.then_inc(h_filled, 1)

            def prologue(layer):
                first = PAIRS * layer
                if layer == 0:
                    pe.wait_ge(wk_split, 1)
                    pe.wait_ge(cT_split, DC)
                    project_k(0, "prologue")
                    pe.wait_ge(cT_split, DC * BATCH)
                    for j in range(1, NK):
                        project_k(j, "prologue")
                    pe.wait_ge(k_split, 1)
                transpose_z(layer, 0, "prologue")
                pe.wait_ge(wv_split, first + 1)
                if layer == 0:
                    pe.wait_ge(k_split, 2)
                project_v(0, "prologue")
                if layer == 0:
                    pe.wait_ge(cols_copied, 2)
                project_v(1, "prologue")
                if layer == 0:
                    pe.wait_ge(k_split, 3)
                transpose_z(layer, 1, "prologue")
                pe.wait_ge(wq_split, first + 1)
                pe.wait_ge(h_split, BATCH * layer + 1)
                project_q(0, "prologue", 0)
                if layer == 0:
                    pe.wait_ge(k_split, 4)
                project_q(1, "prologue", 0)
                pe.wait_ge(v_summed, NV * first + 1)
                project_v(2, "prologue")
                pe.wait_ge(h_split, BATCH * (layer + 1))
                for h in range(NQ):
                    project_q(h, "prologue", 1)
                project_v(3, "prologue")
                if layer == 0:
                    pe.wait_ge(zeros_ready, 1)
                clear_acc(layer)

            def step(pair, last=False, final=False):
                nxt = pair + 1
                pe.wait_ge(q_split, NQ * pair + 1)
                pe.wait_ge(k_split, NK * nxt)
                scores(0, 0)
                pe.wait_ge(v_summed, NV * pair + 3)
                scores(0, 1)
                scores(1, 0)
                pe.wait_ge(q_split, NQ * nxt)
                scores(1, 1)
                if not final:
                    pe.wait_ge(wk_split, pair + 2)
                    project_k(0, "step")
                pe.wait_ge(exp_done, NS * pair + 1)
                scores(2, 0)
                pe.wait_ge(exp_done, NS * pair + 2)
                scores(2, 1)
                pe.wait_ge(exp_done, NS * pair + 3)
                if not final:
                    project_k(1, "step")
                pe.wait_ge(exp_done, NS * pair + 4)
                pe.wait_ge(p_ready, NS * pair + 2)
                transpose_p(0)
                if not final:
                    pe.wait_ge(k_split, NK * nxt + 1)
                transpose_p(1)
                pe.wait_ge(exp_done, NS * pair + 5)
                scores(3, 0)
                pe.wait_ge(exp_done, NS * pair + 6)
                scores(3, 1)
                if not last:
                    pe.wait_ge(k_split, NK * nxt + 2)
                    pe.wait_ge(wq_split, pair + 2)
                    project_q(0, "step")
                pe.wait_ge(v_split, NV * nxt)
                pe.wait_ge(pT_split, NT * pair + 2)
                context(0)
                pe.wait_ge(p_ready, NS * pair + 4)
                transpose_p(2)
                transpose_p(3)
                if not final:
                    pe.wait_ge(exp_done, NS * pair + 7)
                    project_k(2, "step")
                    pe.wait_ge(exp_done, NS * pair + 8)
                    project_k(3, "step")
                pe.wait_ge(o_split, NU * pair + 1)
                pe.wait_ge(pT_split, NT * pair + 4)
                context(1)
                pe.wait_ge(p_ready, NS * pair + 6)
                if not last:
                    pe.wait_ge(q_split, NQ * nxt + 1)
                transpose_p(4)
                transpose_p(5)
                if not last:
                    project_q(1, "step")
                pe.wait_ge(o_split, NU * pair + 2)
                pe.wait_ge(wo_split, pair + 1)
                output(0)
                pe.wait_ge(pT_split, NT * pair + 6)
                context(2)
                pe.wait_ge(p_ready, NS * pair + 8)
                if not final:
                    pe.wait_ge(k_split, NK * nxt + 3)
                transpose_p(6)
                if not final:
                    pe.wait_ge(k_split, NK * nxt + 4)
                transpose_p(7)
                if not last:
                    pe.wait_ge(wv_split, pair + 2)
                    project_v(0, "step")
                    project_v(1, "step")
                pe.wait_ge(o_split, NU * pair + 3)
                if last:
                    output(1, batches=[0], stop=True)
                pe.wait_ge(pT_split, NT * pair + 8)
                context(3)
                if not last:
                    pe.wait_ge(q_split, NQ * nxt + 2)
                    project_v(2, "step")
                pe.wait_ge(o_split, NU * nxt)
                if last:
                    output(1, batches=[1], stop=True)
                else:
                    project_v(3, "step")
                    output(1)

            pe.wait_ge(ident_ready, 2)
            for j in range(DC * BATCH):
                b, c = divmod(j, DC)
                pe.wait_ge(c_loaded[b], LOAD)
                for t in range(CTB):
                    last = pe.transpose(ring[j][:, t * P:(t + 1) * P], c_raw[:, CTB * b + t, c * P:(c + 1) * P], ident[:])
                last.then_inc(cT_filled, 1)
            pe.wait_ge(rows_loaded, 2 * LOAD)
            pe.transpose(ring[4][:, 0:P], head_rows[:], ident[:])
            pe.transpose(ring[4][:, P:P + 20], dim_rows[:], ident[0:20, 0:20]).then_inc(cols_filled, 1)
            for layer in range(LAYERS):
                prologue(layer)
                with pe.Fori(PAIRS * layer, PAIRS * (layer + 1) - 1) as pair:
                    step(pair)
                step(PAIRS * (layer + 1) - 1, last=True, final=layer == LAYERS - 1)

            def hidden_layer(f, b=None):
                if f < 2:
                    w_hi, w_lo, cols = wk_hi, wk_lo, slice(f * P, (f + 1) * P)
                    pe.wait_ge(wk_split, ALL_PAIRS + 1)
                else:
                    w_hi, w_lo, cols = wf1_hi, wf1_lo, slice((f - 2) * P, (f - 1) * P)
                    pe.wait_ge(wf_split, f // 2)
                if f >= 5:
                    pe.wait_ge(gelu_done, f - 4)
                part = slice(0, TOK) if b is None else slice(b * QLEN, (b + 1) * QLEN)
                last = product(ring[G_BANKS[f]][:, part], [(w_hi[:, c, cols], w_lo[:, c, cols], h_hi[:, c, part], h_lo[:, c, part])
                                                           for c in range(DC)])
                if b != 0:
                    last.then_inc(g_filled, 1)

            def mlp_output(f):
                pe.wait_ge(g_split, f + 1)
                pe.wait_ge(wf_split, 4 + f // 2)
                for t in range(QT):
                    toks = slice(t * P, (t + 1) * P)
                    last = product(acc[t // 2][:, (t % 2) * D:(t % 2 + 1) * D],
                                   [(hidden(k_hi, v_hi, f)[:, toks], hidden(k_lo, v_lo, f)[:, toks], wf2_hi[:, f, :], wf2_lo[:, f, :])],
                                   start=False, stop=f == FT - 1 and t % 2 == 1)
                    if f == FT - 1 and t % 2 == 1:
                        last.then_inc(acc_filled, 1)

            transpose_z(LAYERS, 0, "mlp")
            clear_acc(LAYERS)
            pe.wait_ge(h_split, BATCH * LAYERS + 1)
            for f in range(BY_BATCH):
                hidden_layer(f, 0)
            transpose_z(LAYERS, 1, "mlp")
            pe.wait_ge(h_split, BATCH * NORMS)
            for f in range(BY_BATCH):
                hidden_layer(f, 1)
            for f in range(2, FT + 2):
                if BY_BATCH <= f < FT:
                    hidden_layer(f)
                mlp_output(f - 2)


def kernel(**inputs):
    import numpy as np
    import concourse.bacc as bacc
    from concourse.bass_utils import run_bass_kernel_spmd

    def a(name):
        return np.asarray(inputs["L0_xattn_" + name])

    def heads(name):
        return [a(f"{name}{layer}").reshape(HEADS, HD) for layer in (1, 2)]

    arrays = {
        "x_in": np.asarray(inputs["x"]),
        "ctx_in": np.asarray(inputs["ctx_2048"]),
        "wq_in": np.concatenate([a("wq1"), a("wq2")], axis=1),
        "wk_in": np.concatenate([a("wk1"), a("wk2"), a("w_fc1")[:, :PW]], axis=1),
        "wv_in": np.concatenate([a("wv1"), a("wv2")], axis=1),
        "wo_in": np.concatenate([a("wo1"), a("wo2")], axis=0),
        "vrows_in": np.stack([np.concatenate([a("bv1"), a("bv2")]),
                              np.concatenate([a("bias_v1").ravel(), a("bias_v2").ravel()])]),
        "head_rows_in": np.concatenate(heads("bq") + heads("bk") + heads("bias_v") + heads("bias_k"), axis=0),
        "dim_rows_in": np.concatenate([a(n) for n in ("ln1_scale", "ln1_offset", "ln2_scale", "ln2_offset",
                                                      "ln_mlp_scale", "ln_mlp_offset", "b_fc1")]).reshape(20, P),
        "out_rows_in": np.stack([a("bo1"), a("bo2"), a("b_fc2")]),
        "wf1_in": np.ascontiguousarray(a("w_fc1")[:, PW:]),
        "wf2_in": a("w_fc2"),
    }
    arrays = {name: np.ascontiguousarray(v) for name, v in arrays.items()}
    nc = bacc.Bacc("TRN2", target_bir_lowering=False, num_devices=1)
    args = [nc.dram_tensor(name, v.shape, mybir.dt.from_np(v.dtype), kind="ExternalInput").ap() for name, v in arrays.items()]
    args.append(nc.dram_tensor("out", (BATCH, QLEN, D), F32, kind="ExternalOutput").ap())
    build_program(nc, *args)
    result = run_bass_kernel_spmd(nc, [arrays], core_ids=[0])
    return result.results[0]["out"]
```

```python
from contextlib import ExitStack

import concourse.bass as bass
from concourse import mybir

F32 = mybir.dt.float32
F32R = mybir.dt.float32r
ALU = mybir.AluOpType
ACT = mybir.ActivationFunctionType
AX_X = mybir.AxisListType.X

P = 128
BATCH, QLEN, CLEN, D = 2, 256, 512, 256
HEADS, HD, F = 16, 128, 1024
LAYERS = 2
LN_EPS = 1e-5
SCALE = float(HD) ** -0.5

DC = D // P
TOK = BATCH * QLEN
QT = TOK // P
QTB = QLEN // P
CT = BATCH * CLEN // P
CTB = CLEN // P
PW = 2 * HD
PAIRS = HEADS // 2
ALL_PAIRS = LAYERS * PAIRS
FT = F // P
FB = F - PW
NORMS = LAYERS + 1
UNITS = {"step": [(0, 0), (0, 1), (1, 0), (1, 1)], "final": [(0, 0), (1, 0), (0, 1), (1, 1)]}
UNITS["last"] = UNITS["step"]
NU = len(UNITS["step"])
NS = NU * QTB
NT = NU * 2
NK = 2 * BATCH
NQ = 2
NV = CT // 2
BQ, BK, BV, BIAS_K = 0, 1, 2, 3
CTX_BANK = 5
S_BANKS = {"step": [0, 1, 2, 3, 0, CTX_BANK, 2, 0], "final": [0, 1, 2, 3, 4, 0, 1, 2]}
PT_BANKS = {"step": [3, 4, 3, 4, 1, 3, 2, 0], "final": [3, 4, CTX_BANK, 0, 4, 1, 2, CTX_BANK]}
O_BANKS = {"step": [CTX_BANK] * NU, "last": [CTX_BANK, CTX_BANK, CTX_BANK, 3], "final": [3, 0, 3, 4]}
K_BANKS = {"step": [4, 1, 2, 0], "last": [4, 1, 1, 2], "prologue": [0, 1, 2, 3]}
Q_BANKS = {"step": [1, 4], "prologue": [0, 2]}
V_BANKS = {"step": [1, 3, 4, CTX_BANK], "prologue": [1, 4, 3, CTX_BANK]}
H_BANKS = {"prologue": [0, 2], "mlp": [1, CTX_BANK]}
NG = BATCH * FT
G_BANKS = [(n + 2) % 5 for n in range(NG)]
G_LAG = 3
WARM_UP, KEEP_WARM = 6, 3
LOAD = 16


def build_program(nc, x_in, ctx_in, wq_in, wk_in, wv_in, wo_in, vrows_in, head_rows_in,
                  dim_rows_in, out_rows_in, wf1_in, wf2_in, out):
    with ExitStack() as stack:
        def sb(name, shape, dt=F32):
            return stack.enter_context(nc.sbuf_tensor(name, shape, dt))

        def sem(name):
            return stack.enter_context(nc.semaphore(name))

        ring = [stack.enter_context(nc.psum_tensor(f"ring{i}", [P, 512], F32)) for i in range(5)]
        ring.append(stack.enter_context(nc.psum_tensor("ps_ctx", [P, 512], F32)))
        acc = [stack.enter_context(nc.psum_tensor(f"acc{i}", [P, 512], F32)) for i in range(2)]

        ident = sb("ident", [P, P])
        zeros = sb("zeros", [P, 512], F32R)
        minus_half = sb("minus_half", [P, QT])
        head_rows = sb("head_rows", [P, P])
        dim_rows = sb("dim_rows", [20, P])
        head_cols = sb("head_cols", [P, 4, LAYERS * HEADS])
        step_cols = sb("step_cols", [P, ALL_PAIRS + 1, 3, 2])
        cols = sb("cols", [P, 3, 2])
        dim_cols = sb("dim_cols", [P, 20])
        table_load = sb("table_load", [P, 1])
        out_rows = sb("out_rows", [P, NORMS, D])
        cT_hi = sb("cT_hi", [P, DC, CT * P], F32R)
        cT_lo = sb("cT_lo", [P, DC, CT * P], F32R)
        x_sb = sb("x_sb", [P, QT, D])
        x_res = sb("x_res", [P, QT, D])
        z_sb = sb("z_sb", [P, QT, D])
        h_full = sb("h_full", [P, DC, TOK])
        h_hi = sb("h_hi", [P, DC, TOK], F32R)
        h_lo = sb("h_lo", [P, DC, TOK], F32R)
        bn = sb("bn", [P, QT, 6])
        mean_var = sb("mean_var", [P, QT, 2])
        var_eps = sb("var_eps", [P, QT])
        rstd = sb("rstd", [P, QT])
        wq_raw = sb("wq_raw", [P, DC, PW])
        wk_raw = sb("wk_raw", [P, DC, PW])
        wv_raw = sb("wv_raw", [P, DC, PW])
        wo_raw = sb("wo_raw", [P, 2, D])
        wq_hi, wq_lo = sb("wq_hi", [P, DC, PW], F32R), sb("wq_lo", [P, DC, PW], F32R)
        wk_hi, wk_lo = sb("wk_hi", [P, DC, PW], F32R), sb("wk_lo", [P, DC, PW], F32R)
        wv_hi, wv_lo = sb("wv_hi", [P, DC, PW], F32R), sb("wv_lo", [P, DC, PW], F32R)
        wo_hi, wo_lo = sb("wo_hi", [P, 2, D], F32R), sb("wo_lo", [P, 2, D], F32R)
        vrows = sb("vrows", [P, 2, PW])
        vbias = sb("vbias", [P, PW])
        q_hi, q_lo = sb("q_hi", [P, 2, TOK], F32R), sb("q_lo", [P, 2, TOK], F32R)
        k_hi, k_lo = sb("k_hi", [P, 2, CT * P], F32R), sb("k_lo", [P, 2, CT * P], F32R)
        v_sum = sb("v_sum", [P, 2, 2 * PW])
        v_hi, v_lo = sb("v_hi", [P, CT, PW], F32R), sb("v_lo", [P, CT, PW], F32R)
        probs = sb("probs", [P, NU, QTB, CLEN])
        row_max = sb("row_max", [P, NU, QTB])
        shift = sb("shift", [P, NU, QTB])
        p_learned = sb("p_learned", [P, NU, QTB])
        row_sum = sb("row_sum", [P, NU, QTB])
        total = sb("total", [P, NU, QTB])
        inv = sb("inv", [P, NU, QTB])
        pT_hi, pT_lo = sb("pT_hi", [P, 2, CTB, QLEN], F32R), sb("pT_lo", [P, 2, CTB, QLEN], F32R)
        o_hi, o_lo = sb("o_hi", [P, 2, TOK], F32R), sb("o_lo", [P, 2, TOK], F32R)
        wf_raw = sb("wf_raw", [P, 2, 512])
        wf1_hi, wf1_lo = sb("wf1_hi", [P, DC, FB], F32R), sb("wf1_lo", [P, DC, FB], F32R)
        wf2_hi, wf2_lo = sb("wf2_hi", [P, FT, D], F32R), sb("wf2_lo", [P, FT, D], F32R)

        def g_full(n):
            return v_sum[:, n // 2 % 2, n % 2 * QLEN:(n % 2 + 1) * QLEN]

        c_raw = probs[:].rearrange("p u q t -> p (u q t)")[:, 0:CT * D].rearrange("p (t d) -> p t d", d=D)

        def hidden(part_k, part_v, n):
            part = part_k[:].rearrange("p h t -> p (h t)") if n < NG // 2 else part_v[:].rearrange("p t c -> p (t c)")
            return part[:, n % (NG // 2) * QLEN:(n % (NG // 2) + 1) * QLEN]

        c_loaded = [sem(f"c_loaded{b}") for b in range(BATCH)]
        x_loaded, rows_loaded, out_rows_loaded = sem("x_loaded"), sem("rows_loaded"), sem("out_rows_loaded")
        wq_loaded, wk_loaded, wv_loaded, wo_loaded = (sem(f"w{n}_loaded") for n in "qkvo")
        wq_split, wk_split, wv_split, wo_split = (sem(f"w{n}_split") for n in "qkvo")
        wq_rounded, wk_rounded, wv_rounded, wo_rounded = (sem(f"w{n}_rounded") for n in "qkvo")
        wf_loaded = [sem(f"wf_loaded{i}") for i in range(2)]
        wf_rounded, wf_split = sem("wf_rounded"), sem("wf_split")
        ident_ready, zeros_ready = sem("ident_ready"), sem("zeros_ready")
        cT_filled, cT_rounded, cT_split = sem("cT_filled"), sem("cT_rounded"), sem("cT_split")
        cols_filled, cols_copied, cols_ready = sem("cols_filled"), sem("cols_copied"), sem("cols_ready")
        x_ready, bn_done, stats_ready = sem("x_ready"), sem("bn_done"), sem("stats_ready")
        eps_added, rstd_ready, z_ready = sem("eps_added"), sem("rstd_ready"), sem("z_ready")
        h_filled, h_drained, h_rounded, h_split = (sem(f"h_{n}") for n in ("filled", "drained", "rounded", "split"))
        res_ready = sem("res_ready")
        k_filled, k_rounded, k_split = sem("k_filled"), sem("k_rounded"), sem("k_split")
        q_filled, q_rounded, q_split = sem("q_filled"), sem("q_rounded"), sem("q_split")
        v_filled, v_summed, v_rounded, v_split = (sem(f"v_{n}") for n in ("filled", "summed", "rounded", "split"))
        s_filled, max_done, shift_ready = sem("s_filled"), sem("max_done"), sem("shift_ready")
        exp_done, total_done, inv_ready, p_ready = sem("exp_done"), sem("total_done"), sem("inv_ready"), sem("p_ready")
        pT_filled, pT_rounded, pT_split = sem("pT_filled"), sem("pT_rounded"), sem("pT_split")
        o_filled, o_rounded, o_split = sem("o_filled"), sem("o_rounded"), sem("o_split")
        acc_filled = sem("acc_filled")
        g_filled, gelu_done, g_rounded, g_split = (sem(f"g_{n}") for n in ("filled", "gelu", "rounded", "split"))
        passed, stored = sem("passed"), sem("stored")

        block = stack.enter_context(nc.Block())

        @block.sync
        def _(sp):
            def load_wk(n):
                sp.dma_start(wk_raw[:], wk_in[:, bass.ds(n * PW, PW)].rearrange("(c p) n -> p c n", p=P)).then_inc(wk_loaded, LOAD)

            def load_wq(n):
                sp.dma_start(wq_raw[:], wq_in[:, bass.ds(n * PW, PW)].rearrange("(c p) n -> p c n", p=P)).then_inc(wq_loaded, LOAD)

            def load_wv(n):
                sp.dma_start(wv_raw[:], wv_in[:, bass.ds(n * PW, PW)].rearrange("(c p) n -> p c n", p=P)).then_inc(wv_loaded, LOAD)
                sp.dma_start(vrows[:], vrows_in[:, bass.ds(n * PW, PW)].rearrange("(o r) n -> o r n", o=1).to_broadcast([P, 2, PW])).then_inc(wv_loaded, LOAD)

            def load_wo(n):
                sp.dma_start(wo_raw[:], wo_in[bass.ds(n * PW, PW), :].rearrange("(h p) n -> p h n", p=P)).then_inc(wo_loaded, LOAD)

            c_view = ctx_in.rearrange("b (t p) d -> p (b t) d", p=P)
            for b in range(BATCH):
                tiles = slice(CTB * b, CTB * (b + 1))
                sp.dma_start(c_raw[:, tiles, :], c_view[:, tiles, :]).then_inc(c_loaded[b], LOAD)
                if b == 0:
                    load_wk(0)
            sp.dma_start(head_rows[:], head_rows_in).then_inc(rows_loaded, LOAD)
            sp.dma_start(dim_rows[:], dim_rows_in).then_inc(rows_loaded, LOAD)
            sp.dma_start(x_sb[:], x_in.rearrange("b (t p) d -> p (b t) d", p=P)).then_inc(x_loaded, LOAD)
            load_wv(0)
            load_wq(0)
            load_wo(0)
            sp.dma_start(out_rows[:], out_rows_in.rearrange("(o r) n -> o r n", o=1).to_broadcast([P, NORMS, D])).then_inc(out_rows_loaded, LOAD)
            sp.wait_ge(wk_split, 1)
            load_wk(1)
            sp.wait_ge(wv_split, 1)
            load_wv(1)
            sp.wait_ge(wq_split, 1)
            load_wq(1)
            sp.wait_ge(wk_split, 2)
            load_wk(2)

            def refill(pair, wq=True, wk=True):
                if wq:
                    sp.wait_ge(wq_split, pair + 2)
                    load_wq(pair + 2)
                    sp.wait_ge(wv_split, pair + 2)
                    load_wv(pair + 2)
                sp.wait_ge(wo_split, pair + 1)
                load_wo(pair + 1)
                if wk:
                    sp.wait_ge(wk_split, pair + 3)
                    load_wk(pair + 3)

            def load_mlp(part):
                if part < 3:
                    src = wf1_in[:, PW * part:PW * (part + 1)].rearrange("(c p) n -> p c n", p=P)
                    dst = wf_raw[:, part % 2, :].rearrange("p (c n) -> p c n", c=DC)
                else:
                    src = wf2_in[PW * (part - 3):PW * (part - 2), :].rearrange("(f p) n -> p f n", p=P)
                    dst = wf_raw[:, part % 2, :].rearrange("p (f n) -> p f n", n=D)
                if part >= 2:
                    sp.wait_ge(wf_split, part - 1)
                sp.dma_start(dst, src).then_inc(wf_loaded[part % 2], LOAD)

            load_mlp(0)
            load_mlp(1)
            with sp.Fori(0, PAIRS - 1) as pair:
                refill(pair)
            refill(PAIRS - 1)
            for part in range(2, 5):
                load_mlp(part)
            with sp.Fori(PAIRS, ALL_PAIRS - 2) as pair:
                refill(pair)
            refill(ALL_PAIRS - 2, wq=False, wk=False)
            for part in range(5, 7):
                load_mlp(part)

            for b in range(BATCH):
                tiles = slice(QTB * b, QTB * (b + 1))
                sp.wait_ge(x_ready, BATCH * LAYERS + b + 1)
                sp.dma_start(out.rearrange("b (t p) d -> p (b t) d", p=P)[:, tiles, :], x_sb[:, tiles, :]).then_inc(stored, LOAD)
            sp.wait_ge(stored, BATCH * LOAD)

        @block.gpsimd
        def _(pool):
            def hold(semaphore, value):
                pool.wait_ge(semaphore, value)
                pool.sem_inc(passed, 1)

            def split_tile(raw, hi, lo, rounded, n, done):
                pool.tensor_scalar(hi, raw, 1.0, 0.0, ALU.mult, ALU.add).then_inc(rounded, 1)
                pool.wait_ge(rounded, n)
                pool.tensor_tensor(lo, raw, hi.bitcast(F32), ALU.subtract).then_inc(done, 1)

            def split_wk(n):
                hold(wk_loaded, (n + 1) * LOAD)
                split_tile(wk_raw[:], wk_hi[:], wk_lo[:], wk_rounded, n + 1, wk_split)

            def split_wq(n):
                hold(wq_loaded, (n + 1) * LOAD)
                split_tile(wq_raw[:], wq_hi[:], wq_lo[:], wq_rounded, n + 1, wq_split)

            def value_bias(n):
                pool.wait_ge(wv_loaded, (2 * n + 2) * LOAD)
                pool.tensor_tensor(vbias[:], vrows[:, 0, :], vrows[:, 1, :], ALU.subtract)

            def split_wv(n):
                split_tile(wv_raw[:], wv_hi[:], wv_lo[:], wv_rounded, n + 1, wv_split)

            def split_wo(n):
                hold(wo_loaded, (n + 1) * LOAD)
                split_tile(wo_raw[:], wo_hi[:], wo_lo[:], wo_rounded, n + 1, wo_split)

            def split_mlp(part):
                pool.wait_ge(wf_loaded[part % 2], (part // 2 + 1) * LOAD)
                if part < 3:
                    hi = wf1_hi[:, :, PW * part:PW * (part + 1)]
                    lo = wf1_lo[:, :, PW * part:PW * (part + 1)]
                    raw = wf_raw[:, part % 2, :].rearrange("p (c n) -> p c n", c=DC)
                else:
                    f = 2 * (part - 3)
                    hi, lo = wf2_hi[:, f:f + 2, :], wf2_lo[:, f:f + 2, :]
                    raw = wf_raw[:, part % 2, :].rearrange("p (f n) -> p f n", n=D)
                split_tile(raw, hi, lo, wf_rounded, part + 1, wf_split)

            def inverse_deviation(norm, b):
                tiles = slice(QTB * b, QTB * (b + 1))
                half = BATCH * norm + b + 1
                pool.wait_ge(stats_ready, half)
                pool.tensor_scalar(var_eps[:, tiles], mean_var[:, tiles, 1], 1.0, LN_EPS, ALU.mult, ALU.add).then_inc(eps_added, 1)
                pool.wait_ge(eps_added, half)
                pool.tensor_tensor(rstd[:, tiles], var_eps[:, tiles], minus_half[:, tiles], ALU.pow).then_inc(rstd_ready, 1)

            def residual(norm):
                rows = out_rows[:, norm:norm + 1, :].to_broadcast([P, QT, D])
                pool.tensor_tensor(x_res[:], x_sb[:], rows, ALU.add).then_inc(res_ready, 1)

            def value_rest(pair, m):
                pool.wait_ge(v_rounded, NV * pair + m + 1)
                pool.tensor_tensor(v_lo[:, 2 * m:2 * m + 2, :], v_sum[:, m % 2, :].rearrange("p (t c) -> p t c", c=PW),
                                   v_hi[:, 2 * m:2 * m + 2, :].bitcast(F32), ALU.subtract).then_inc(v_split, 1)

            def normalise(pair, u):
                hold(inv_ready, NU * pair + u + 1)
                for q in range(QTB):
                    pool.tensor_scalar(probs[:, u, q, :], probs[:, u, q, :], inv[:, u, q:q + 1], 0.0, ALU.mult, ALU.add).then_inc(p_ready, 1)

            pool.memset(zeros[:].bitcast(F32), 0.0).then_inc(zeros_ready, 1)
            pool.memset(ident[:], 0.0).then_inc(ident_ready, 1)
            pool.memset(minus_half[:], -0.5)
            pool.wait_ge(ident_ready, 1)
            pool.affine_select(out=ident[:], in_=ident[:], compare_op=ALU.not_equal, fill=1.0, base=0,
                               pattern=[[-1, P]], channel_multiplier=1).then_inc(ident_ready, 1)
            split_wk(0)
            pool.wait_ge(cols_copied, 2)
            by_pair = head_cols[:].rearrange("p g (n h) -> p g n h", h=2)
            pool.memset(step_cols[:, 0, BV, :], 0.0)
            pool.memset(step_cols[:, ALL_PAIRS, 0:2, :], 0.0)
            pool.tensor_tensor(step_cols[:, 0:ALL_PAIRS, BK, :], by_pair[:, BK], by_pair[:, BIAS_K], ALU.subtract)
            pool.tensor_copy(step_cols[:, 0:ALL_PAIRS, BQ, :], by_pair[:, BQ])
            pool.tensor_copy(step_cols[:, 1:ALL_PAIRS + 1, BV, :], by_pair[:, BV]).then_inc(cols_ready, 1)

            def prologue(layer):
                first = PAIRS * layer
                if layer == 0:
                    value_bias(0)
                    inverse_deviation(0, 0)
                    split_wv(0)
                    inverse_deviation(0, 1)
                    split_wq(0)
                    pool.wait_ge(k_filled, NK)
                    split_wk(1)
                else:
                    inverse_deviation(layer, 0)
                    inverse_deviation(layer, 1)
                    split_mlp(2)
                for m in range(NV):
                    value_rest(first, m)

            def step(pair, last=False, final=False):
                if final:
                    pool.wait_ge(s_filled, NS * pair + 1)
                    split_wo(pair)
                normalise(pair, 0)
                if not final:
                    pool.wait_ge(q_filled, NQ * (pair + 1))
                    split_wq(pair + 1)
                normalise(pair, 1)
                if not final:
                    pool.wait_ge(v_summed, NV * (pair + 1))
                    value_bias(pair + 1)
                    split_wv(pair + 1)
                normalise(pair, 2)
                if not final:
                    pool.wait_ge(s_filled, NS * pair + 1)
                    split_wo(pair)
                normalise(pair, 3)
                if not final:
                    pool.wait_ge(k_filled, NK * (pair + 2))
                    split_wk(pair + 2)
                if not last:
                    for m in range(NV):
                        value_rest(pair + 1, m)

            prologue(0)
            with pool.Fori(0, PAIRS - 1) as pair:
                step(pair)
            step(PAIRS - 1, last=True)
            pool.wait_ge(out_rows_loaded, LOAD)
            residual(0)
            split_mlp(0)
            split_mlp(1)
            prologue(1)
            with pool.Fori(PAIRS, ALL_PAIRS - 1) as pair:
                step(pair)
            step(ALL_PAIRS - 1, last=True, final=True)
            residual(1)
            split_mlp(3)
            inverse_deviation(LAYERS, 0)
            split_mlp(4)
            split_mlp(5)
            inverse_deviation(LAYERS, 1)
            split_mlp(6)
            residual(LAYERS)

        @block.scalar
        def _(act):
            def column(group, pair, h, where):
                return cols[:, group, h:h + 1] if where != "prologue" else step_cols[:, pair, group, h:h + 1]

            def round_k(pair, j, where):
                h, b = divmod(j, BATCH)
                act.wait_ge(k_filled, NK * pair + j + 1)
                act.activation(k_hi[:, h, b * CLEN:(b + 1) * CLEN], ring[K_BANKS[where][j]][:], ACT.Identity,
                               bias=column(BK, pair, h, where)).then_inc(k_rounded, 1)

            def round_q(pair, h, where):
                act.wait_ge(q_filled, NQ * pair + h + 1)
                act.activation(q_hi[:, h, :], ring[Q_BANKS[where][h]][:], ACT.Identity,
                               bias=column(BQ, pair, h, where)).then_inc(q_rounded, 1)

            def round_v(pair, m):
                act.wait_ge(v_summed, NV * pair + m + 1)
                act.activation(v_hi[:, 2 * m:2 * m + 2, :], v_sum[:, m % 2, :].rearrange("p (t c) -> p t c", c=PW),
                               ACT.Copy).then_inc(v_rounded, 1)

            def round_pT(pair, j, where="step"):
                u, half = divmod(j, 2)
                act.wait_ge(pT_filled, NT * pair + j + 1)
                act.activation(pT_hi[:, u % 2, 2 * half:2 * half + 2, :],
                               ring[PT_BANKS[where][j]][:].rearrange("p (t q) -> p t q", q=QLEN), ACT.Copy).then_inc(pT_rounded, 1)

            def round_o(pair, u, where="step"):
                h, b = UNITS[where][u]
                act.wait_ge(o_filled, NU * pair + u + 1)
                act.activation(o_hi[:, h, b * QLEN:(b + 1) * QLEN], ring[O_BANKS[where][u]][:, 0:QLEN], ACT.Identity,
                               bias=cols[:, BV, h:h + 1]).then_inc(o_rounded, 1)

            def exponential(pair, u, q, where="step"):
                act.wait_ge(shift_ready, NS * pair + QTB * u + q + 1)
                if q == QTB - 1:
                    act.activation(p_learned[:, u, :], shift[:, u, :], ACT.Exp)
                act.activation(probs[:, u, q, :], ring[S_BANKS[where][QTB * u + q]][:], ACT.Exp, bias=shift[:, u, q:q + 1],
                               scale=SCALE, accum_out=row_sum[:, u, q:q + 1]).then_inc(exp_done, 1)

            def exponentials(pair, u, where="step"):
                for q in range(QTB):
                    exponential(pair, u, q, where)

            def round_h(norm, b):
                part = slice(b * QLEN, (b + 1) * QLEN)
                for c in range(DC):
                    act.wait_ge(h_drained, DC * (BATCH * norm + b) + c + 1)
                    act.activation(h_hi[:, c, part], h_full[:, c, part], ACT.Copy).then_inc(h_rounded, 1)

            def prologue(layer):
                first = PAIRS * layer
                if layer == 0:
                    for j in range(NK):
                        round_k(first, j, "prologue")
                round_v(first, 0)
                round_h(layer, 0)
                round_h(layer, 1)
                round_v(first, 1)
                round_q(first, 0, "prologue")
                round_v(first, 2)
                round_q(first, 1, "prologue")
                round_v(first, 3)

            def step(pair, last=False):
                exponentials(pair, 0)
                round_k(pair + 1, 0, "step")
                exponentials(pair, 1)
                round_k(pair + 1, 1, "step")
                exponential(pair, 2, 0)
                round_pT(pair, 0)
                round_pT(pair, 1)
                exponential(pair, 2, 1)
                if not last:
                    round_q(pair + 1, 0, "step")
                else:
                    round_k(pair + 1, 2, "last")
                round_pT(pair, 2)
                exponential(pair, 3, 0)
                round_pT(pair, 3)
                if last:
                    round_o(pair, 0)
                    exponential(pair, 3, 1)
                else:
                    exponential(pair, 3, 1)
                    round_o(pair, 0)
                if not last:
                    round_k(pair + 1, 2, "step")
                round_k(pair + 1, 3, "last" if last else "step")
                round_o(pair, 1)
                round_pT(pair, 4)
                round_pT(pair, 5)
                if last:
                    round_pT(pair, 6)
                    round_pT(pair, 7)
                    round_o(pair, 2, "last")
                    round_o(pair, 3, "last")
                    return
                round_q(pair + 1, 1, "step")
                round_o(pair, 2)
                round_pT(pair, 6)
                round_pT(pair, 7)
                round_v(pair + 1, 0)
                round_v(pair + 1, 1)
                round_o(pair, 3)
                round_v(pair + 1, 2)
                round_v(pair + 1, 3)

            def final_step(pair):
                exponentials(pair, 0, "final")
                exponentials(pair, 1, "final")
                exponential(pair, 2, 0, "final")
                round_pT(pair, 0, "final")
                exponential(pair, 2, 1, "final")
                round_pT(pair, 1, "final")
                round_pT(pair, 2, "final")
                round_pT(pair, 3, "final")
                exponentials(pair, 3, "final")
                round_o(pair, 0, "final")
                round_pT(pair, 4, "final")
                round_pT(pair, 5, "final")
                round_o(pair, 1, "final")
                round_pT(pair, 6, "final")
                round_pT(pair, 7, "final")
                act.activation(table_load[:], dim_cols[:, 0:1], ACT.Gelu)
                round_o(pair, 2, "final")
                round_o(pair, 3, "final")

            for j in range(DC * BATCH):
                b, c = divmod(j, DC)
                act.wait_ge(cT_filled, j + 1)
                act.activation(cT_hi[:, c, b * CLEN:(b + 1) * CLEN], ring[j][:], ACT.Copy).then_inc(cT_rounded, 1)
            act.wait_ge(cols_ready, 1)
            for layer in range(LAYERS):
                prologue(layer)
                with act.Fori(PAIRS * layer, PAIRS * (layer + 1) - 1) as pair:
                    step(pair)
                if layer < LAYERS - 1:
                    step(PAIRS * (layer + 1) - 1, last=True)
            final_step(ALL_PAIRS - 1)
            round_h(LAYERS, 0)
            for n in range(NG):
                if n == 3:
                    round_h(LAYERS, 1)
                f = n % FT
                act.wait_ge(g_filled, n + 1)
                if n >= 4:
                    act.wait_ge(g_split, n - 3)
                act.activation(g_full(n), ring[G_BANKS[n]][:, 0:QLEN], ACT.Gelu,
                               bias=dim_cols[:, 4 * NORMS + f:4 * NORMS + f + 1]).then_inc(gelu_done, 1)

        @block.vector
        def _(dve):
            def column(group, pair, h, where):
                return cols[:, group, h:h + 1] if where != "prologue" else step_cols[:, pair, group, h:h + 1]

            def split_k(pair, j, where):
                h, b = divmod(j, BATCH)
                part = slice(b * CLEN, (b + 1) * CLEN)
                dve.wait_ge(k_rounded, NK * pair + j + 1)
                dve.scalar_tensor_tensor(out=k_lo[:, h, part], in0=ring[K_BANKS[where][j]][:],
                                         scalar=column(BK, pair, h, where),
                                         in1=k_hi[:, h, part].bitcast(F32), op0=ALU.add, op1=ALU.subtract).then_inc(k_split, 1)

            def split_q(pair, h, where):
                dve.wait_ge(q_rounded, NQ * pair + h + 1)
                dve.scalar_tensor_tensor(out=q_lo[:, h, :], in0=ring[Q_BANKS[where][h]][:],
                                         scalar=column(BQ, pair, h, where),
                                         in1=q_hi[:, h, :].bitcast(F32), op0=ALU.add, op1=ALU.subtract).then_inc(q_split, 1)

            def sum_v(pair, m, where):
                dve.wait_ge(v_filled, NV * pair + m + 1)
                if not isinstance(pair, int) or NV * pair + m >= 2:
                    dve.wait_ge(v_split, NV * pair + m - 1)
                dve.tensor_tensor(v_sum[:, m % 2, :].rearrange("p (t c) -> p t c", c=PW),
                                  ring[V_BANKS[where][m]][:].rearrange("p (t c) -> p t c", c=PW),
                                  vbias[:].rearrange("p (o c) -> p o c", o=1).to_broadcast([P, 2, PW]), ALU.add).then_inc(v_summed, 1)

            def split_pT(pair, j, where="step"):
                u, half = divmod(j, 2)
                dve.wait_ge(pT_rounded, NT * pair + j + 1)
                dve.tensor_tensor(pT_lo[:, u % 2, 2 * half:2 * half + 2, :],
                                  ring[PT_BANKS[where][j]][:].rearrange("p (t q) -> p t q", q=QLEN),
                                  pT_hi[:, u % 2, 2 * half:2 * half + 2, :].bitcast(F32), ALU.subtract).then_inc(pT_split, 1)

            def split_o(pair, u, where="step"):
                h, b = UNITS[where][u]
                part = slice(b * QLEN, (b + 1) * QLEN)
                dve.wait_ge(o_rounded, NU * pair + u + 1)
                dve.scalar_tensor_tensor(out=o_lo[:, h, part], in0=ring[O_BANKS[where][u]][:, 0:QLEN],
                                         scalar=cols[:, BV, h:h + 1],
                                         in1=o_hi[:, h, part].bitcast(F32), op0=ALU.add, op1=ALU.subtract).then_inc(o_split, 1)

            def maximum(pair, u, q, where="step"):
                dve.wait_ge(s_filled, NS * pair + QTB * u + q + 1)
                dve.reduce_max(row_max[:, u, q:q + 1], ring[S_BANKS[where][QTB * u + q]][:], AX_X).then_inc(max_done, 1)

            def shifts(pair, u, tiles=range(QTB)):
                part = slice(tiles[0], tiles[-1] + 1)
                dve.wait_ge(max_done, NS * pair + QTB * u + tiles[-1] + 1)
                dve.tensor_scalar(shift[:, u, part], row_max[:, u, part], -SCALE, 0.0, ALU.mult, ALU.min).then_inc(shift_ready, len(tiles))

            def maxima(pair, u, where="step"):
                for q in range(QTB):
                    maximum(pair, u, q, where)
                    if u == 0:
                        shifts(pair, u, range(q, q + 1))
                if u > 0:
                    shifts(pair, u)

            def inverse_sums(pair, u):
                dve.wait_ge(exp_done, NS * pair + QTB * (u + 1))
                dve.tensor_tensor(total[:, u, :], row_sum[:, u, :], p_learned[:, u, :], ALU.add).then_inc(total_done, 1)
                dve.wait_ge(total_done, NU * pair + u + 1)
                dve.reciprocal(inv[:, u, :], total[:, u, :]).then_inc(inv_ready, 1)

            def new_x(n, b):
                dve.wait_ge(acc_filled, BATCH * n + b + 1)
                dve.wait_ge(res_ready, n + 1)
                dve.tensor_tensor(x_sb[:, QTB * b:QTB * (b + 1), :], acc[b][:].rearrange("p (t d) -> p t d", d=D),
                                  x_res[:, QTB * b:QTB * (b + 1), :], ALU.add).then_inc(x_ready, 1)

            def stats(norm, b):
                if norm > 0:
                    dve.wait_ge(x_ready, BATCH * (norm - 1) + b + 1)
                for t in range(QTB * b, QTB * (b + 1)):
                    dve.bn_stats(bn[:, t, :], x_sb[:, t, :]).then_inc(bn_done, 1)
                dve.wait_ge(bn_done, QT * norm + QTB * (b + 1))
                for t in range(QTB * b, QTB * (b + 1)):
                    agg = dve.bn_aggr(mean_var[:, t, :], bn[:, t, :])
                agg.then_inc(stats_ready, 1)

            def standardise(norm, b):
                dve.wait_ge(stats_ready, BATCH * norm + b + 1)
                dve.wait_ge(rstd_ready, BATCH * norm + b + 1)
                for t in range(QTB * b, QTB * (b + 1)):
                    dve.tensor_scalar(z_sb[:, t, :], x_sb[:, t, :], mean_var[:, t, 0:1], rstd[:, t:t + 1],
                                      ALU.subtract, ALU.mult).then_inc(z_ready, 1)

            def scale_h(norm, b, where):
                dve.wait_ge(h_filled, BATCH * norm + b + 1)
                for c in range(DC):
                    dve.tensor_scalar(h_full[:, c, b * QLEN:(b + 1) * QLEN], ring[H_BANKS[where][b]][:, c * QLEN:(c + 1) * QLEN],
                                      dim_cols[:, 4 * norm + c:4 * norm + c + 1],
                                      dim_cols[:, 4 * norm + DC + c:4 * norm + DC + c + 1], ALU.mult, ALU.add).then_inc(h_drained, 1)

            def split_h(norm, b):
                part = slice(b * QLEN, (b + 1) * QLEN)
                dve.wait_ge(h_rounded, DC * (BATCH * norm + b + 1))
                dve.tensor_tensor(h_lo[:, :, part], h_full[:, :, part], h_hi[:, :, part].bitcast(F32), ALU.subtract).then_inc(h_split, 1)

            def prologue(layer):
                first = PAIRS * layer
                if layer == 0:
                    dve.wait_ge(x_loaded, LOAD)
                    stats(0, 0)
                    stats(0, 1)
                    split_k(first, 0, "prologue")
                    standardise(0, 0)
                    split_k(first, 1, "prologue")
                    split_k(first, 2, "prologue")
                    split_k(first, 3, "prologue")
                    standardise(layer, 1)
                else:
                    standardise(layer, 0)
                dve.wait_ge(wv_split, first + 1)
                sum_v(first, 0, "prologue")
                if layer > 0:
                    standardise(layer, 1)
                scale_h(layer, 0, "prologue")
                scale_h(layer, 1, "prologue")
                split_h(layer, 0)
                split_h(layer, 1)
                sum_v(first, 1, "prologue")
                sum_v(first, 2, "prologue")
                split_q(first, 0, "prologue")
                sum_v(first, 3, "prologue")
                split_q(first, 1, "prologue")

            def copy_cols(pair):
                dve.tensor_copy(cols[:].rearrange("p g h -> p (g h)"),
                                step_cols[:, bass.ds(pair + 1, 1), :, :].rearrange("p n g h -> p (n g h)"))

            def step(pair, last=False):
                copy_cols(pair)
                maxima(pair, 0)
                maxima(pair, 1)
                inverse_sums(pair, 0)
                split_k(pair + 1, 0, "step")
                maxima(pair, 2)
                inverse_sums(pair, 1)
                split_k(pair + 1, 1, "step")
                maximum(pair, 3, 0)
                split_pT(pair, 0)
                split_pT(pair, 1)
                maximum(pair, 3, 1)
                shifts(pair, 3)
                inverse_sums(pair, 2)
                if not last:
                    split_q(pair + 1, 0, "step")
                else:
                    split_k(pair + 1, 2, "last")
                split_pT(pair, 2)
                split_pT(pair, 3)
                if last:
                    split_o(pair, 0)
                    inverse_sums(pair, 3)
                else:
                    inverse_sums(pair, 3)
                    split_o(pair, 0)
                if not last:
                    split_k(pair + 1, 2, "step")
                split_k(pair + 1, 3, "last" if last else "step")
                split_o(pair, 1)
                split_pT(pair, 4)
                split_pT(pair, 5)
                if last:
                    split_pT(pair, 6)
                    split_pT(pair, 7)
                    split_o(pair, 2, "last")
                    split_o(pair, 3, "last")
                    for b in range(BATCH):
                        new_x((pair + 1) // PAIRS - 1, b)
                        stats((pair + 1) // PAIRS, b)
                    return
                split_q(pair + 1, 1, "step")
                split_o(pair, 2)
                split_pT(pair, 6)
                split_pT(pair, 7)
                dve.wait_ge(wv_split, pair + 2)
                sum_v(pair + 1, 0, "step")
                sum_v(pair + 1, 1, "step")
                split_o(pair, 3)
                sum_v(pair + 1, 2, "step")
                sum_v(pair + 1, 3, "step")

            def final_step(pair):
                copy_cols(pair)
                maxima(pair, 0, "final")
                maxima(pair, 1, "final")
                inverse_sums(pair, 0)
                maxima(pair, 2, "final")
                inverse_sums(pair, 1)
                maxima(pair, 3, "final")
                split_pT(pair, 0, "final")
                inverse_sums(pair, 2)
                split_pT(pair, 1, "final")
                split_pT(pair, 2, "final")
                split_pT(pair, 3, "final")
                inverse_sums(pair, 3)
                split_o(pair, 0, "final")
                split_pT(pair, 4, "final")
                split_pT(pair, 5, "final")
                split_o(pair, 1, "final")
                split_pT(pair, 6, "final")
                split_pT(pair, 7, "final")
                new_x(LAYERS - 1, 0)
                stats(LAYERS, 0)
                split_o(pair, 2, "final")
                standardise(LAYERS, 0)
                split_o(pair, 3, "final")

            for j in range(DC * BATCH):
                b, c = divmod(j, DC)
                part = slice(b * CLEN, (b + 1) * CLEN)
                dve.wait_ge(cT_rounded, j + 1)
                dve.tensor_tensor(cT_lo[:, c, part], ring[j][:], cT_hi[:, c, part].bitcast(F32), ALU.subtract).then_inc(cT_split, 1)
            dve.wait_ge(cols_filled, 1)
            dve.tensor_copy(head_cols[:].rearrange("p g c -> p (g c)"), ring[4][:, 0:P]).then_inc(cols_copied, 1)
            dve.tensor_copy(dim_cols[:], ring[4][:, P:P + 20]).then_inc(cols_copied, 1)
            dve.wait_ge(cols_ready, 1)
            for layer in range(LAYERS):
                prologue(layer)
                with dve.Fori(PAIRS * layer, PAIRS * (layer + 1) - 1) as pair:
                    step(pair)
                if layer < LAYERS - 1:
                    step(PAIRS * (layer + 1) - 1, last=True)
            final_step(ALL_PAIRS - 1)
            scale_h(LAYERS, 0, "mlp")
            new_x(LAYERS - 1, 1)
            split_h(LAYERS, 0)
            stats(LAYERS, 1)
            for n in range(NG):
                if n == 1:
                    standardise(LAYERS, 1)
                if n == 2:
                    scale_h(LAYERS, 1, "mlp")
                if n == 3:
                    split_h(LAYERS, 1)
                if n == FT + G_LAG + 1:
                    new_x(LAYERS, 0)
                dve.wait_ge(gelu_done, n + 1)
                dve.tensor_copy(hidden(k_hi, v_hi, n), g_full(n)).then_inc(g_rounded, 1)
                dve.wait_ge(g_rounded, n + 1)
                dve.tensor_tensor(hidden(k_lo, v_lo, n), g_full(n), hidden(k_hi, v_hi, n).bitcast(F32),
                                  ALU.subtract).then_inc(g_split, 1)
            new_x(LAYERS, 1)

        @block.tensor
        def _(pe):
            def product(out_ap, terms, start=True, stop=True):
                passes = [(a, b) for lhs_hi, lhs_lo, rhs_hi, rhs_lo in terms
                          for a, b in ((lhs_hi, rhs_lo), (lhs_lo, rhs_hi), (lhs_hi, rhs_hi))]
                for i, (a, b) in enumerate(passes):
                    ins = pe.matmul(out_ap, a, b, start=start and i == 0, stop=stop and i == len(passes) - 1)
                return ins

            def project_k(j, where):
                h, b = divmod(j, BATCH)
                cols, part = slice(h * HD, (h + 1) * HD), slice(b * CLEN, (b + 1) * CLEN)
                product(ring[K_BANKS[where][j]][:], [(wk_hi[:, c, cols], wk_lo[:, c, cols], cT_hi[:, c, part], cT_lo[:, c, part])
                                                     for c in range(DC)]).then_inc(k_filled, 1)

            def project_q(h, where, b=None):
                cols = slice(h * HD, (h + 1) * HD)
                part = slice(0, TOK) if b is None else slice(b * QLEN, (b + 1) * QLEN)
                last = product(ring[Q_BANKS[where][h]][:, part], [(wq_hi[:, c, cols], wq_lo[:, c, cols], h_hi[:, c, part], h_lo[:, c, part])
                                                                  for c in range(DC)])
                if b != 0:
                    last.then_inc(q_filled, 1)

            def project_v(m, where):
                for i in range(2):
                    toks = slice((2 * m + i) * P, (2 * m + i + 1) * P)
                    last = product(ring[V_BANKS[where][m]][:, i * PW:(i + 1) * PW],
                                   [(cT_hi[:, c, toks], cT_lo[:, c, toks], wv_hi[:, c, :], wv_lo[:, c, :]) for c in range(DC)])
                last.then_inc(v_filled, 1)

            def scores(u, q, where="step"):
                h, b = UNITS[where][u]
                toks, part = slice(b * QLEN + q * P, b * QLEN + (q + 1) * P), slice(b * CLEN, (b + 1) * CLEN)
                product(ring[S_BANKS[where][QTB * u + q]][:], [(q_hi[:, h, toks], q_lo[:, h, toks], k_hi[:, h, part], k_lo[:, h, part])]).then_inc(s_filled, 1)

            def transpose_p(j, where="step"):
                u, half = divmod(j, 2)
                for t in range(2):
                    for q in range(QTB):
                        src = (2 * half + t) * P
                        last = pe.transpose(ring[PT_BANKS[where][j]][:, t * QLEN + q * P:t * QLEN + (q + 1) * P],
                                            probs[:, u, q, src:src + P], ident[:])
                last.then_inc(pT_filled, 1)

            def context(u, where="step"):
                h, b = UNITS[where][u]
                cols = slice(h * HD, (h + 1) * HD)
                product(ring[O_BANKS[where][u]][:, 0:QLEN],
                        [(v_hi[:, CTB * b + t, cols], v_lo[:, CTB * b + t, cols], pT_hi[:, u % 2, t, :], pT_lo[:, u % 2, t, :])
                         for t in range(CTB)]).then_inc(o_filled, 1)

            def output(h, b, stop=False):
                for t in range(QTB):
                    toks = slice(b * QLEN + t * P, b * QLEN + (t + 1) * P)
                    last = product(acc[b][:, t * D:(t + 1) * D], [(o_hi[:, h, toks], o_lo[:, h, toks], wo_hi[:, h, :], wo_lo[:, h, :])],
                                   start=False, stop=stop and t == QTB - 1)
                if stop:
                    last.then_inc(acc_filled, 1)

            def keep_warm(n):
                for _ in range(n):
                    pe.matmul(ring[4][:], zeros[:, 0:P], zeros[:], start=True, stop=True)

            def clear_acc(n, b):
                if n > 0:
                    pe.wait_ge(x_ready, BATCH * (n - 1) + b + 1)
                pe.matmul(acc[b][:], zeros[:, 0:P], zeros[:], start=True, stop=False)

            def transpose_z(norm, b, where):
                pe.wait_ge(z_ready, QT * norm + QTB * (b + 1))
                for c in range(DC):
                    for t in range(QTB):
                        last = pe.transpose(ring[H_BANKS[where][b]][:, c * QLEN + t * P:c * QLEN + (t + 1) * P],
                                            z_sb[:, QTB * b + t, c * P:(c + 1) * P], ident[:])
                last.then_inc(h_filled, 1)

            def prologue(layer):
                first = PAIRS * layer
                if layer == 0:
                    pe.wait_ge(wk_split, 1)
                    pe.wait_ge(cT_split, DC)
                    project_k(0, "prologue")
                    pe.wait_ge(cT_split, DC * BATCH)
                    for j in range(1, NK):
                        project_k(j, "prologue")
                    pe.wait_ge(k_split, 1)
                    transpose_z(0, 0, "prologue")
                    pe.wait_ge(wv_split, 1)
                    pe.wait_ge(k_split, 2)
                    project_v(0, "prologue")
                    pe.wait_ge(cols_copied, 2)
                    project_v(1, "prologue")
                    pe.wait_ge(k_split, 3)
                    transpose_z(0, 1, "prologue")
                    pe.wait_ge(k_split, 4)
                    project_v(2, "prologue")
                else:
                    pe.wait_ge(wv_split, first + 1)
                    for m in range(3):
                        project_v(m, "prologue")
                    transpose_z(layer, 0, "prologue")
                    transpose_z(layer, 1, "prologue")
                project_v(3, "prologue")
                pe.wait_ge(wq_split, first + 1)
                for b in range(BATCH):
                    pe.wait_ge(h_split, BATCH * layer + b + 1)
                    project_q(0, "prologue", b)
                for b in range(BATCH):
                    clear_acc(layer, b)
                for b in range(BATCH):
                    project_q(1, "prologue", b)

            def step(pair, last=False):
                nxt = pair + 1
                pe.wait_ge(q_split, NQ * pair + 1)
                pe.wait_ge(k_split, NK * nxt)
                scores(0, 0)
                pe.wait_ge(v_summed, NV * pair + 1)
                scores(0, 1)
                pe.wait_ge(q_split, NQ * nxt)
                scores(1, 0)
                pe.wait_ge(v_summed, NV * pair + 3)
                scores(1, 1)
                pe.wait_ge(wk_split, pair + 2)
                project_k(0, "step")
                pe.wait_ge(exp_done, NS * pair + 1)
                scores(2, 0)
                pe.wait_ge(v_split, NV * nxt)
                scores(2, 1)
                pe.wait_ge(exp_done, NS * pair + 2)
                project_k(1, "step")
                pe.wait_ge(exp_done, NS * pair + 4)
                pe.wait_ge(p_ready, NS * pair + 2)
                transpose_p(0)
                pe.wait_ge(k_split, NK * nxt + 1)
                transpose_p(1)
                scores(3, 0)
                pe.wait_ge(exp_done, NS * pair + 5)
                scores(3, 1)
                pe.wait_ge(k_split, NK * nxt + 2)
                if last:
                    project_k(2, "last")
                else:
                    pe.wait_ge(wq_split, pair + 2)
                    project_q(0, "step")
                pe.wait_ge(p_ready, NS * pair + 4)
                pe.wait_ge(pT_split, NT * pair + 1)
                transpose_p(2)
                pe.wait_ge(pT_split, NT * pair + 2)
                transpose_p(3)
                pe.wait_ge(exp_done, NS * pair + 6)
                context(0)
                pe.wait_ge(exp_done, NS * pair + 7)
                if last:
                    project_k(3, "last")
                else:
                    project_k(2, "step")
                    pe.wait_ge(exp_done, NS * pair + 8)
                    project_k(3, "step")
                pe.wait_ge(o_split, NU * pair + 1)
                pe.wait_ge(pT_split, NT * pair + 4)
                context(1)
                pe.wait_ge(p_ready, NS * pair + 6)
                if last:
                    pe.wait_ge(k_split, NK * nxt + 3)
                else:
                    pe.wait_ge(q_split, NQ * nxt + 1)
                transpose_p(4)
                transpose_p(5)
                if not last:
                    project_q(1, "step")
                pe.wait_ge(wo_split, pair + 1)
                output(0, 0)
                pe.wait_ge(o_split, NU * pair + 2)
                if last:
                    pe.wait_ge(p_ready, NS * pair + 8)
                    pe.wait_ge(exp_done, NS * pair + 8)
                    pe.wait_ge(k_split, NK * (nxt + 1))
                    transpose_p(6)
                    transpose_p(7)
                    pe.wait_ge(pT_split, NT * pair + 6)
                    context(2, "last")
                    pe.wait_ge(pT_split, NT * pair + 8)
                    context(3, "last")
                    output(0, 1)
                    pe.wait_ge(o_split, NU * pair + 3)
                    output(1, 0, stop=True)
                    pe.wait_ge(o_split, NU * nxt)
                    output(1, 1, stop=True)
                    return
                output(0, 1)
                pe.wait_ge(pT_split, NT * pair + 6)
                context(2)
                pe.wait_ge(p_ready, NS * pair + 8)
                pe.wait_ge(k_split, NK * nxt + 3)
                transpose_p(6)
                pe.wait_ge(k_split, NK * nxt + 4)
                transpose_p(7)
                pe.wait_ge(wv_split, pair + 2)
                project_v(0, "step")
                project_v(1, "step")
                pe.wait_ge(o_split, NU * pair + 3)
                pe.wait_ge(pT_split, NT * pair + 8)
                context(3)
                pe.wait_ge(q_split, NQ * nxt + 2)
                project_v(2, "step")
                pe.wait_ge(o_split, NU * nxt)
                project_v(3, "step")
                output(1, 0)
                output(1, 1)

            def final_step(pair):
                nxt = pair + 1
                pe.wait_ge(q_split, NQ * nxt)
                pe.wait_ge(k_split, NK * nxt)
                scores(0, 0, "final")
                pe.wait_ge(v_summed, NV * pair + 3)
                scores(0, 1, "final")
                scores(1, 0, "final")
                scores(1, 1, "final")
                scores(2, 0, "final")
                pe.wait_ge(exp_done, NS * pair + 1)
                scores(2, 1, "final")
                pe.wait_ge(exp_done, NS * pair + 2)
                scores(3, 0, "final")
                pe.wait_ge(exp_done, NS * pair + 3)
                scores(3, 1, "final")
                pe.wait_ge(p_ready, NS * pair + 2)
                pe.wait_ge(exp_done, NS * pair + 4)
                transpose_p(0, "final")
                pe.wait_ge(exp_done, NS * pair + 5)
                transpose_p(1, "final")
                pe.wait_ge(p_ready, NS * pair + 4)
                pe.wait_ge(v_split, NV * nxt)
                transpose_p(2, "final")
                pe.wait_ge(exp_done, NS * pair + 6)
                transpose_p(3, "final")
                pe.wait_ge(pT_split, NT * pair + 2)
                context(0, "final")
                pe.wait_ge(p_ready, NS * pair + 6)
                transpose_p(4, "final")
                pe.wait_ge(exp_done, NS * pair + 7)
                transpose_p(5, "final")
                pe.wait_ge(pT_split, NT * pair + 4)
                context(1, "final")
                pe.wait_ge(exp_done, NS * pair + 8)
                pe.wait_ge(p_ready, NS * pair + 8)
                transpose_p(6, "final")
                transpose_p(7, "final")
                pe.wait_ge(wo_split, pair + 1)
                pe.wait_ge(o_split, NU * pair + 1)
                output(0, 0)
                pe.wait_ge(o_split, NU * pair + 2)
                output(1, 0, stop=True)
                pe.wait_ge(pT_split, NT * pair + 6)
                context(2, "final")
                pe.wait_ge(pT_split, NT * pair + 8)
                context(3, "final")
                pe.wait_ge(o_split, NU * pair + 3)
                output(0, 1)
                transpose_z(LAYERS, 0, "mlp")
                pe.wait_ge(o_split, NU * nxt)
                output(1, 1, stop=True)

            pe.wait_ge(zeros_ready, 1)
            keep_warm(WARM_UP)
            pe.wait_ge(ident_ready, 2)
            for j in range(DC * BATCH):
                b, c = divmod(j, DC)
                pe.wait_ge(c_loaded[b], LOAD)
                for t in range(CTB):
                    last = pe.transpose(ring[j][:, t * P:(t + 1) * P], c_raw[:, CTB * b + t, c * P:(c + 1) * P], ident[:])
                last.then_inc(cT_filled, 1)
            pe.wait_ge(rows_loaded, 2 * LOAD)
            pe.transpose(ring[4][:, 0:P], head_rows[:], ident[:])
            pe.transpose(ring[4][:, P:P + 20], dim_rows[:], ident[0:20, 0:20]).then_inc(cols_filled, 1)
            for layer in range(LAYERS):
                prologue(layer)
                with nc.Fori(PAIRS * layer, PAIRS * (layer + 1) - 1, engines=(mybir.EngineType.PE,), hint_back_edge=True) as pair:
                    step(pair)
                if layer < LAYERS - 1:
                    step(PAIRS * (layer + 1) - 1, last=True)
            final_step(ALL_PAIRS - 1)

            def hidden_layer(n):
                b, f = divmod(n, FT)
                if f < 2:
                    w_hi, w_lo, cols = wk_hi, wk_lo, slice(f * P, (f + 1) * P)
                    pe.wait_ge(wk_split, ALL_PAIRS + 1)
                else:
                    w_hi, w_lo, cols = wf1_hi, wf1_lo, slice((f - 2) * P, (f - 1) * P)
                    pe.wait_ge(wf_split, f // 2)
                if n >= 5:
                    pe.wait_ge(gelu_done, n - 4)
                part = slice(b * QLEN, (b + 1) * QLEN)
                product(ring[G_BANKS[n]][:, 0:QLEN], [(w_hi[:, c, cols], w_lo[:, c, cols], h_hi[:, c, part], h_lo[:, c, part])
                                                      for c in range(DC)]).then_inc(g_filled, 1)

            def mlp_output(n):
                b, f = divmod(n, FT)
                pe.wait_ge(g_split, n + 1)
                pe.wait_ge(wf_split, 4 + f // 2)
                for t in range(QTB):
                    toks = slice(t * P, (t + 1) * P)
                    last = product(acc[b][:, t * D:(t + 1) * D],
                                   [(hidden(k_hi, v_hi, n)[:, toks], hidden(k_lo, v_lo, n)[:, toks], wf2_hi[:, f, :], wf2_lo[:, f, :])],
                                   start=False, stop=f == FT - 1 and t == QTB - 1)
                if f == FT - 1:
                    last.then_inc(acc_filled, 1)

            clear_acc(LAYERS, 0)
            keep_warm(KEEP_WARM)
            pe.wait_ge(h_split, BATCH * LAYERS + 1)
            for n in range(NG + G_LAG):
                if n == 4:
                    transpose_z(LAYERS, 1, "mlp")
                    clear_acc(LAYERS, 1)
                if n == FT:
                    pe.wait_ge(h_split, BATCH * NORMS)
                if n < NG:
                    hidden_layer(n)
                if n >= G_LAG:
                    mlp_output(n - G_LAG)

def kernel(**inputs):
    import numpy as np
    import concourse.bacc as bacc
    from concourse.bass_utils import run_bass_kernel_spmd

    def a(name):
        return np.asarray(inputs["L0_xattn_" + name])

    def heads(name):
        return [a(f"{name}{layer}").reshape(HEADS, HD) for layer in (1, 2)]

    arrays = {
        "x_in": np.asarray(inputs["x"]),
        "ctx_in": np.asarray(inputs["ctx_2048"]),
        "wq_in": np.concatenate([a("wq1"), a("wq2")], axis=1),
        "wk_in": np.concatenate([a("wk1"), a("wk2"), a("w_fc1")[:, :PW]], axis=1),
        "wv_in": np.concatenate([a("wv1"), a("wv2")], axis=1),
        "wo_in": np.concatenate([a("wo1"), a("wo2")], axis=0),
        "vrows_in": np.stack([np.concatenate([a("bv1"), a("bv2")]),
                              np.concatenate([a("bias_v1").ravel(), a("bias_v2").ravel()])]),
        "head_rows_in": np.concatenate(heads("bq") + heads("bk") + heads("bias_v") + heads("bias_k"), axis=0),
        "dim_rows_in": np.concatenate([a(n) for n in ("ln1_scale", "ln1_offset", "ln2_scale", "ln2_offset",
                                                      "ln_mlp_scale", "ln_mlp_offset", "b_fc1")]).reshape(20, P),
        "out_rows_in": np.stack([a("bo1"), a("bo2"), a("b_fc2")]),
        "wf1_in": np.ascontiguousarray(a("w_fc1")[:, PW:]),
        "wf2_in": a("w_fc2"),
    }
    arrays = {name: np.ascontiguousarray(v) for name, v in arrays.items()}
    nc = bacc.Bacc("TRN2", target_bir_lowering=False, num_devices=1)
    args = [nc.dram_tensor(name, v.shape, mybir.dt.from_np(v.dtype), kind="ExternalInput").ap() for name, v in arrays.items()]
    args.append(nc.dram_tensor("out", (BATCH, QLEN, D), F32, kind="ExternalOutput").ap())
    build_program(nc, *args)
    result = run_bass_kernel_spmd(nc, [arrays], core_ids=[0])
    return result.results[0]["out"]
```
